# Optimizing a Trainium2 kernel written in Bass

```python
import numpy as np
import jax
import jax.numpy as jnp

def _softmax(x, axis=-1):
    return jax.nn.softmax(x, axis=axis)

def _gelu(x):
    return jax.nn.gelu(x, approximate=True)

def _silu(x):
    return jax.nn.silu(x)

def _sigmoid(x):
    return jax.nn.sigmoid(x)

def _layernorm(x, axis=-1, eps=1e-05):
    m = jnp.mean(x, axis=axis, keepdims=True)
    v = jnp.var(x, axis=axis, keepdims=True)
    return (x - m) / jnp.sqrt(v + eps)

def _scatter_add(tgt, idx, src, axis=0):
    return tgt.at[idx].add(src)

def _segment_sum(src, seg, n):
    return jax.ops.segment_sum(src, seg, n)
kernel_name = 'mk_vit_tower_d2_tok_img256_r4_b7e58d'

def setup_inputs(seed: int=0):
    np.random.seed(seed)
    _w = jnp.asarray

    def _rec_inputs():
        import jax
        import jax.numpy as jnp
        _rk = jax.random.key(seed)
        x = -4.65018e-05 + 0.999886 * jax.random.normal(jax.random.fold_in(_rk, 1), (8, 3, 128, 128), jnp.float32)
        return x
    x = _rec_inputs()

    def _L0_tok_setup():
        import jax, jax.numpy as jnp
        import numpy as np
        B, C, H, P, D = (64, 3, 128, 16, 64)
        NP = H // P
        key = jax.random.key(seed)
        ks = jax.random.split(key, 7)
        s = lambda fan_in: 1.0 / np.sqrt(fan_in)
        return {'x': jax.random.normal(ks[0], (B, C, H, H), dtype=jnp.float32), 'Wp': jax.random.normal(ks[1], (P * P * C, D), dtype=jnp.float32) * s(P * P * C), 'bp': jax.random.normal(ks[2], (D,), dtype=jnp.float32) * 0.01, 'W1': jax.random.normal(ks[3], (2, D), dtype=jnp.float32) * s(2), 'b1': jax.random.normal(ks[4], (D,), dtype=jnp.float32) * 0.01, 'W2': jax.random.normal(ks[5], (D, D), dtype=jnp.float32) * s(D), 'b2': jax.random.normal(ks[6], (D,), dtype=jnp.float32) * 0.01}
    _L0_tok_all = _L0_tok_setup()
    _L0_tok_in = {k: v for k, v in _L0_tok_all.items() if k in ('Wp', 'bp', 'W1', 'b1', 'W2', 'b2')}
    del _L0_tok_all

    def _L0_attn_setup():
        import jax, jax.numpy as jnp
        import numpy as np
        import math
        N_SEQ, L_RES, D_MODEL = (128, 96, 64)
        N_HEAD, C_HEAD = (8, 32)
        EPS = 1e-05
        key = jax.random.key(seed)
        ks = jax.random.split(key, 8)
        s = 1.0 / math.sqrt(D_MODEL)
        return {'m': jax.random.normal(ks[0], (N_SEQ, L_RES, D_MODEL), jnp.float32), 'gamma': jnp.ones((D_MODEL,), jnp.float32), 'beta': jnp.zeros((D_MODEL,), jnp.float32), 'Wq': jax.random.normal(ks[1], (D_MODEL, N_HEAD * C_HEAD), jnp.float32) * s, 'Wk': jax.random.normal(ks[2], (D_MODEL, N_HEAD * C_HEAD), jnp.float32) * s, 'Wv': jax.random.normal(ks[3], (D_MODEL, N_HEAD * C_HEAD), jnp.float32) * s, 'Wg': jax.random.normal(ks[4], (D_MODEL, N_HEAD * C_HEAD), jnp.float32) * s, 'bg': jnp.zeros((N_HEAD * C_HEAD,), jnp.float32), 'Wo': jax.random.normal(ks[5], (N_HEAD * C_HEAD, D_MODEL), jnp.float32) * s, 'bo': jnp.zeros((D_MODEL,), jnp.float32)}
    _L0_attn_all = _L0_attn_setup()
    _L0_attn_in = {k: v for k, v in _L0_attn_all.items() if k in ('gamma', 'beta', 'Wq', 'Wk', 'Wv', 'Wg', 'bg', 'Wo', 'bo')}
    del _L0_attn_all

    def _L0_ffn_setup():
        import jax, jax.numpy as jnp
        import numpy as np
        D_IN, D_HID, D_OUT = (64, 128, 64)
        N_EXPERTS, TOP_K = (64, 2)
        B, S = (8, 1024)
        key = jax.random.key(seed)
        ks = jax.random.split(key, 8)
        scale_in = 1.0 / np.sqrt(D_IN)
        scale_hid = 1.0 / np.sqrt(D_HID)
        return {'x': jax.random.normal(ks[0], (B, S, D_IN), dtype=jnp.float32), 'Wr': jax.random.uniform(ks[1], (D_IN, N_EXPERTS), jnp.float32, -scale_in, scale_in), 'br': jax.random.uniform(ks[2], (N_EXPERTS,), jnp.float32, -scale_in, scale_in), 'W1': jax.random.uniform(ks[3], (N_EXPERTS, D_IN, D_HID), jnp.float32, -scale_in, scale_in), 'b1': jax.random.uniform(ks[4], (N_EXPERTS, D_HID), jnp.float32, -scale_in, scale_in), 'W2': jax.random.uniform(ks[5], (N_EXPERTS, D_HID, D_OUT), jnp.float32, -scale_hid, scale_hid), 'b2': jax.random.uniform(ks[6], (N_EXPERTS, D_OUT), jnp.float32, -scale_hid, scale_hid)}
    _L0_ffn_all = _L0_ffn_setup()
    _L0_ffn_in = {k: v for k, v in _L0_ffn_all.items() if k in ('Wr', 'br', 'W1', 'b1', 'W2', 'b2')}
    del _L0_ffn_all

    def _L1_attn_setup():
        import jax, jax.numpy as jnp
        import numpy as np
        MEMORY_SIZE = 40
        INPUT_SIZE = 64
        OUTPUT_SIZE = 64
        BATCH = 16
        SEQ = 1024
        key = jax.random.key(seed)
        k1, k2, k3, k4 = jax.random.split(key, 4)
        x = jax.random.normal(k1, (BATCH, SEQ, INPUT_SIZE), dtype=jnp.float32)
        lim_w = float(np.sqrt(6.0 / (INPUT_SIZE + OUTPUT_SIZE)))
        W1 = jax.random.uniform(k2, (INPUT_SIZE, OUTPUT_SIZE), minval=-lim_w, maxval=lim_w, dtype=jnp.float32)
        W2 = jax.random.uniform(k3, (INPUT_SIZE, OUTPUT_SIZE), minval=-lim_w, maxval=lim_w, dtype=jnp.float32)
        bias = jnp.ones((OUTPUT_SIZE,), dtype=jnp.float32)
        lim_m = float(np.sqrt(6.0 / (MEMORY_SIZE + 1 + INPUT_SIZE)))
        mw = jax.random.uniform(k4, (MEMORY_SIZE + 1, INPUT_SIZE), minval=-lim_m, maxval=lim_m, dtype=jnp.float32)
        mw = mw.at[0].set(0.0)
        return {'input_data': x, 'W1': W1, 'W2': W2, 'bias': bias, 'memory_weights': mw}
    _L1_attn_all = _L1_attn_setup()
    _L1_attn_in = {k: v for k, v in _L1_attn_all.items() if k in ('W1', 'W2', 'bias', 'memory_weights')}
    del _L1_attn_all

    def _L1_ffn_setup():
        import jax, jax.numpy as jnp
        import numpy as np
        B, T, IN_DIM = (64, 64, 64)
        HID, OUT_DIM = (128, 64)
        N_LAYERS, N_EXPERTS, N_SHARED = (2, 16, 1)
        key = jax.random.key(seed)
        ks = jax.random.split(key, 10)
        s = 0.02
        x = jax.random.normal(ks[0], (B, T, IN_DIM), dtype=jnp.float32)
        route_id = jax.random.randint(ks[1], (B,), 0, N_EXPERTS)
        Wi = jax.random.normal(ks[2], (HID, IN_DIM), dtype=jnp.float32) * s
        bi = jnp.zeros((HID,), dtype=jnp.float32)
        Wr = jax.random.normal(ks[3], (N_LAYERS, N_EXPERTS, HID, HID), dtype=jnp.float32) * s
        br = jax.random.normal(ks[4], (N_LAYERS, N_EXPERTS, HID), dtype=jnp.float32) * s
        Ws = jax.random.normal(ks[5], (N_LAYERS, N_SHARED, HID, HID), dtype=jnp.float32) * s
        bs = jax.random.normal(ks[6], (N_LAYERS, N_SHARED, HID), dtype=jnp.float32) * s
        Wo = jax.random.normal(ks[7], (OUT_DIM, HID), dtype=jnp.float32) * s
        bo = jnp.zeros((OUT_DIM,), dtype=jnp.float32)
        return {'x': x, 'route_id': route_id, 'Wi': Wi, 'bi': bi, 'Wr': Wr, 'br': br, 'Ws': Ws, 'bs': bs, 'Wo': Wo, 'bo': bo}
    _L1_ffn_all = _L1_ffn_setup()
    _L1_ffn_in = {k: v for k, v in _L1_ffn_all.items() if k in ('route_id', 'Wi', 'bi', 'Wr', 'br', 'Ws', 'bs', 'Wo', 'bo')}
    del _L1_ffn_all
    return {'x': x, 'L0_tok_Wp': _L0_tok_in['Wp'], 'L0_tok_bp': _L0_tok_in['bp'], 'L0_tok_W1': _L0_tok_in['W1'], 'L0_tok_b1': _L0_tok_in['b1'], 'L0_tok_W2': _L0_tok_in['W2'], 'L0_tok_b2': _L0_tok_in['b2'], 'L0_attn_gamma': _L0_attn_in['gamma'], 'L0_attn_beta': _L0_attn_in['beta'], 'L0_attn_Wq': _L0_attn_in['Wq'], 'L0_attn_Wk': _L0_attn_in['Wk'], 'L0_attn_Wv': _L0_attn_in['Wv'], 'L0_attn_Wg': _L0_attn_in['Wg'], 'L0_attn_bg': _L0_attn_in['bg'], 'L0_attn_Wo': _L0_attn_in['Wo'], 'L0_attn_bo': _L0_attn_in['bo'], 'L0_ffn_Wr': _L0_ffn_in['Wr'], 'L0_ffn_br': _L0_ffn_in['br'], 'L0_ffn_W1': _L0_ffn_in['W1'], 'L0_ffn_b1': _L0_ffn_in['b1'], 'L0_ffn_W2': _L0_ffn_in['W2'], 'L0_ffn_b2': _L0_ffn_in['b2'], 'L1_attn_W1': _L1_attn_in['W1'], 'L1_attn_W2': _L1_attn_in['W2'], 'L1_attn_bias': _L1_attn_in['bias'], 'L1_attn_memory_weights': _L1_attn_in['memory_weights'], 'L1_ffn_route_id': _L1_ffn_in['route_id'], 'L1_ffn_Wi': _L1_ffn_in['Wi'], 'L1_ffn_bi': _L1_ffn_in['bi'], 'L1_ffn_Wr': _L1_ffn_in['Wr'], 'L1_ffn_br': _L1_ffn_in['br'], 'L1_ffn_Ws': _L1_ffn_in['Ws'], 'L1_ffn_bs': _L1_ffn_in['bs'], 'L1_ffn_Wo': _L1_ffn_in['Wo'], 'L1_ffn_bo': _L1_ffn_in['bo']}

def reference(x, L0_tok_Wp, L0_tok_bp, L0_tok_W1, L0_tok_b1, L0_tok_W2, L0_tok_b2, L0_attn_gamma, L0_attn_beta, L0_attn_Wq, L0_attn_Wk, L0_attn_Wv, L0_attn_Wg, L0_attn_bg, L0_attn_Wo, L0_attn_bo, L0_ffn_Wr, L0_ffn_br, L0_ffn_W1, L0_ffn_b1, L0_ffn_W2, L0_ffn_b2, L1_attn_W1, L1_attn_W2, L1_attn_bias, L1_attn_memory_weights, L1_ffn_route_id, L1_ffn_Wi, L1_ffn_bi, L1_ffn_Wr, L1_ffn_br, L1_ffn_Ws, L1_ffn_bs, L1_ffn_Wo, L1_ffn_bo):
    import jax
    import jax.numpy as jnp

    def _L0_tok_ref(x, Wp, bp, W1, b1, W2, b2):
        import jax, jax.numpy as jnp
        import numpy as np
        B, C, H, P, D = (64, 3, 128, 16, 64)
        NP = H // P
        b = x.shape[0]
        patches = x.reshape(b, C, NP, P, NP, P)
        patches = patches.transpose(0, 2, 4, 1, 3, 5).reshape(b, NP * NP, C * P * P)
        embedded = jnp.einsum('bnk,kd->bnd', patches, Wp) + bp
        gx, gy = jnp.meshgrid(jnp.arange(NP, dtype=jnp.float32), jnp.arange(NP, dtype=jnp.float32), indexing='ij')
        xy = jnp.stack([gx, gy], axis=-1).reshape(1, -1, 2) / (NP - 1)
        pos = jax.nn.relu(xy @ W1 + b1) @ W2 + b2
        return embedded + pos

    def _L0_attn_ref(m, gamma, beta, Wq, Wk, Wv, Wg, bg, Wo, bo):
        import jax, jax.numpy as jnp
        import numpy as np
        import math
        N_SEQ, L_RES, D_MODEL = (128, 96, 64)
        N_HEAD, C_HEAD = (8, 32)
        EPS = 1e-05
        N, L, D = m.shape
        H, C = (N_HEAD, C_HEAD)
        mu = jnp.mean(m, axis=-1, keepdims=True)
        var = jnp.mean(jnp.square(m - mu), axis=-1, keepdims=True)
        mn = (m - mu) * jax.lax.rsqrt(var + EPS) * gamma + beta
        q = (mn @ Wq).reshape(N, L, H, C)
        k = (mn @ Wk).reshape(N, L, H, C)
        v = (mn @ Wv).reshape(N, L, H, C)
        g = jax.nn.sigmoid(mn @ Wg + bg).reshape(N, L, H, C)
        scale = 1.0 / math.sqrt(C) / math.sqrt(L)
        att = jnp.einsum('slhc,tlhc->sth', q, k) * scale
        att = jax.nn.softmax(att, axis=1)
        o = jnp.einsum('sth,tlhc->slhc', att, v) * g
        return o.reshape(N, L, H * C) @ Wo + bo

    def _L0_ffn_ref(x, Wr, br, W1, b1, W2, b2):
        import jax, jax.numpy as jnp
        import numpy as np
        D_IN, D_HID, D_OUT = (64, 128, 64)
        N_EXPERTS, TOP_K = (64, 2)
        B, S = (8, 1024)
        Bx, Sx, D = x.shape
        xf = x.reshape(-1, D)
        T = xf.shape[0]
        E = Wr.shape[1]
        logits = xf @ Wr + br
        topk_logits, topk_idx = jax.lax.top_k(logits, TOP_K)
        gates = jax.nn.softmax(topk_logits, axis=1)
        combine = jnp.zeros((T, E), xf.dtype).at[jnp.arange(T)[:, None], topk_idx].add(gates)
        out = jnp.zeros((T, W2.shape[-1]), xf.dtype)
        for e in range(E):
            h = jax.nn.relu(xf @ W1[e] + b1[e])
            y = h @ W2[e] + b2[e]
            out = out + combine[:, e:e + 1] * y
        return out.reshape(Bx, Sx, -1)

    def _L1_attn_ref(input_data, W1, W2, bias, memory_weights):
        import jax, jax.numpy as jnp
        import numpy as np
        MEMORY_SIZE = 40
        INPUT_SIZE = 64
        OUTPUT_SIZE = 64
        BATCH = 16
        SEQ = 1024
        m = memory_weights.shape[0] - 1
        B, T, D = input_data.shape
        total = jnp.sum(input_data, axis=1, keepdims=True)
        h_hatt = jnp.zeros_like(input_data)
        win = jnp.zeros_like(input_data)
        for l in range(1, m + 1):
            shifted = jnp.pad(input_data[:, :T - l], ((0, 0), (l, 0), (0, 0)))
            h_hatt = h_hatt + memory_weights[l] * shifted
            win = win + shifted
        h_hatt = h_hatt + memory_weights[0] * (total - win)
        return input_data @ W1 + h_hatt @ W2 + bias

    def _L1_ffn_ref(x, route_id, Wi, bi, Wr, br, Ws, bs, Wo, bo):
        import jax, jax.numpy as jnp
        import numpy as np
        B, T, IN_DIM = (64, 64, 64)
        HID, OUT_DIM = (128, 64)
        N_LAYERS, N_EXPERTS, N_SHARED = (2, 16, 1)
        flat = x.reshape(-1, x.shape[-1])
        n_tok = flat.shape[0]
        route = jnp.repeat(route_id, n_tok // route_id.shape[0])
        h = jax.nn.relu(flat @ Wi.T + bi)
        n_layers, n_experts = (Wr.shape[0], Wr.shape[1])
        for l in range(n_layers):
            shared = (jnp.einsum('nd,shd->snh', h, Ws[l]) + bs[l][:, None, :]).mean(axis=0)
            routed = jnp.zeros_like(h)
            for e in range(n_experts):
                ye = h @ Wr[l, e].T + br[l, e]
                routed = routed + jnp.where((route == e)[:, None], ye, 0.0)
            h = jax.nn.relu(shared + routed + h)
        out = h @ Wo.T + bo
        return out.reshape(*x.shape[:-1], out.shape[-1])
    h = _L0_tok_ref(x, L0_tok_Wp, L0_tok_bp, L0_tok_W1, L0_tok_b1, L0_tok_W2, L0_tok_b2)
    h = h + _L0_attn_ref(_layernorm(h, axis=-1), L0_attn_gamma, L0_attn_beta, L0_attn_Wq, L0_attn_Wk, L0_attn_Wv, L0_attn_Wg, L0_attn_bg, L0_attn_Wo, L0_attn_bo)
    h = h + _L0_ffn_ref(_layernorm(h, axis=-1), L0_ffn_Wr, L0_ffn_br, L0_ffn_W1, L0_ffn_b1, L0_ffn_W2, L0_ffn_b2)
    h = h + _L1_attn_ref(_layernorm(h, axis=-1), L1_attn_W1, L1_attn_W2, L1_attn_bias, L1_attn_memory_weights)
    h = h + _L1_ffn_ref(_layernorm(h, axis=-1), L1_ffn_route_id, L1_ffn_Wi, L1_ffn_bi, L1_ffn_Wr, L1_ffn_br, L1_ffn_Ws, L1_ffn_bs, L1_ffn_Wo, L1_ffn_bo)
    return h

_drawn_inputs = setup_inputs


def setup_inputs(seed=0):
    import zlib

    import numpy as np

    out = dict(_drawn_inputs(seed))
    spreads = {'L0_attn_gamma': (1.0, 0.2),
     'L0_attn_beta': (0.0, 0.1),
     'L0_attn_bg': (0.0, 0.289),
     'L0_attn_bo': (0.0, 0.1),
     'L1_attn_bias': (1.0, 0.2),
     'L1_ffn_bi': (0.0, 0.8),
     'L1_ffn_bo': (0.0, 0.312)}
    factors = {'L0_tok_bp': 3.378,
     'L0_tok_b1': 3.552,
     'L0_tok_b2': 3.127,
     'L0_ffn_b1': 4.066,
     'L1_ffn_Wi': 5.545,
     'L1_ffn_Wr': 8.0,
     'L1_ffn_br': 8.0,
     'L1_ffn_Ws': 8.0,
     'L1_ffn_bs': 8.0,
     'L1_ffn_Wo': 3.293}
    for name, (base, spread) in spreads.items():
        noise = np.random.default_rng([zlib.crc32(name.encode()), seed]).standard_normal(out[name].shape)
        drawn = base * np.exp(spread * noise) if base else spread * noise
        out[name] = jnp.asarray(drawn.astype(out[name].dtype))
    for name, factor in factors.items():
        out[name] = (out[name] * factor).astype(out[name].dtype)
    return out
```

```python
from contextlib import ExitStack

import concourse.bass as bass
from concourse import mybir

F32 = mybir.dt.float32
F32R = mybir.dt.float32r
I32 = mybir.dt.int32
U32 = mybir.dt.uint32
ALU = mybir.AluOpType
ACT = mybir.ActivationFunctionType
AX = mybir.AxisListType

P = 128
B, CH, IMG, PATCH = 8, 3, 128, 16
NP = IMG // PATCH
T = NP * NP
N = B * T
J = N // P
TJ = T // J
D = 64
HEADS, HC = 8, 32
E, HID = 64, 128
TAPS = 40
PAIRS = TAPS // 2 + 1
NL, NE = 2, 16
EPS = 1e-5
SCALE = 1.0 / (HC ** 0.5) / (T ** 0.5)
KP = CH * PATCH
C_ID, C_II, C_IOTA, C_MASK, C_PART = 0, 128, 192, 256, 320
C_COLS = 321


def build_tower(nc, I, out):
    with ExitStack() as ctx:
        def sb(name, shape, dt=F32):
            return ctx.enter_context(nc.sbuf_tensor(name, shape, dt))

        def sem(name):
            return ctx.enter_context(nc.semaphore(name))

        bank = [ctx.enter_context(nc.psum_tensor(f"bank{i}", [P, 512], F32)) for i in range(8)]

        const = sb("const", [P, C_COLS])
        ident = const[:, C_ID:C_ID + P]
        fold = const[:, C_II:C_II + D]
        expert_no = const[:, C_IOTA:C_IOTA + E]
        off_head = const[0:D, C_MASK:C_MASK + D]
        part_no = const[0:NE, C_PART:C_PART + 1]
        grid = sb("grid", [3, N])
        early = sb("early", [P, NP * B * IMG])
        image = early[0:KP, :].rearrange("k (y b w) -> k y b w", y=NP, b=B)
        wp = sb("wp", [KP, PATCH, D])
        pos_w1 = sb("pos_w1", [3, D])
        pos_hid = sb("pos_hid", [D + 2, N])
        pos_w2 = sb("pos_w2", [D + 2, D])
        room = sb("room", [P, 5 * TJ * D])
        emb_half = room[:, 9 * N:10 * N]
        h0 = sb("h0", [P, J, D])
        h0b = sb("h0b", [P, J, D])
        h1 = sb("h1", [P, J, D])
        h2 = sb("h2", [P, J, D])
        h2b = sb("h2b", [P, J, D])
        h3 = sb("h3", [P, J, D])
        h3b = sb("h3b", [P, J, D])
        h4 = sb("h4", [P, J, D])
        stats = sb("stats", [P, J, 6])
        mean_var = sb("mean_var", [P, J, 2])
        var_arg = sb("var_arg", [P, J])
        rstd = sb("rstd", [P, J])
        minus_half = sb("minus_half", [P, J])
        xn = sb("xn", [P, J, 2, D])
        vec_rows = sb("vec_rows", [NL + 3, P])
        vec_t = sb("vec_t", [P, NL + 3])
        gamma = vec_t[0:D, NL + 1:NL + 2]
        beta = vec_t[0:D, NL + 2:NL + 3]
        mn_t = sb("mn_t", [D + 1, N])
        w_qkvg = sb("w_qkvg", [D + 1, 4, HEADS * HC])
        q4 = room[:, 0 * N:2 * N].rearrange("p (l h b) -> p l h b", l=TJ, h=HEADS)
        k4 = room[:, 2 * N:4 * N].rearrange("p (l h b) -> p l h b", l=TJ, h=HEADS)
        v4 = room[:, 4 * N:6 * N].rearrange("p (l h b) -> p l h b", l=TJ, h=HEADS)
        gexp = sb("gexp", [P, HEADS, TJ, B])
        g4 = sb("g4", [P, HEADS, TJ, B])
        vt = room[0:D, 6 * N:10 * N].rearrange("p (l c) -> p l c", l=TJ)
        sm = sb("sm", [D, D])
        sm_max = sb("sm_max", [D, 1])
        sm_bias = sb("sm_bias", [D, 1])
        sm_exp = sb("sm_exp", [D, D])
        sm_sum = sb("sm_sum", [D, 1])
        sm_rec = sb("sm_rec", [D, 1])
        att = sb("att", [D, D])
        att_t = sb("att_t", [D, D])
        o4 = gexp
        wo_diag = sb("wo_diag", [P, HEADS, P])
        wo_out = sb("wo_out", [P, 2, P])
        bo_row = sb("bo_row", [P, D])
        wr = sb("wr", [D + 1, E])
        x2_t = room[:, 8 * N:9 * N]
        x2_one = sb("x2_one", [D + 1, N])
        x_ab = sb("x_ab", [P, 2, N], F32R)
        w1_raw = sb("w1_raw", [P, E // 2, HID])
        w1_hl = sb("w1_hl", [P, E, HID], F32R)
        w2e = sb("w2e", [HID, E, D])
        b1_raw = sb("b1_raw", [E, HID])
        b1_t = sb("b1_t", [HID, E])
        b2e = sb("b2e", [E, D])
        logits = sb("logits", [P, J, E])
        top8 = sb("top8", [P, J, 8])
        top_i = sb("top_i", [P, J, 8], U32)
        top_f = sb("top_f", [P, J, 2])
        gap = sb("gap", [P, J])
        gap_exp = sb("gap_exp", [P, J])
        gate_sum = sb("gate_sum", [P, J])
        gate = sb("gate", [P, 2, J])
        comb1 = sb("comb1", [P, J, E])
        comb2 = sb("comb2", [P, J, E])
        comb = sb("comb", [P, J, 2, E])
        c_t = room[:, 9 * N:10 * N]
        c_high = sb("c_high", [P, N], F32R)
        c_hl = sb("c_hl", [P, N], F32R)
        fold_r = sb("fold_r", [P, D], F32R)
        hb = early[:, 0:4 * N].rearrange("p (u n) -> p u n", u=4)
        hg = early[:, 4 * N:8 * N].rearrange("p (u n) -> p u n", u=4)
        half = early[:, 15 * N:16 * N]
        w2c = sb("w2c", [P, D])
        mw_rows = sb("mw_rows", [PAIRS + 1, P])
        mw_t = sb("mw_t", [P, PAIRS + 1])
        mw_rel = sb("mw_rel", [P, PAIRS])
        wc = sb("wc", [P, PAIRS, D])
        w_total = sb("w_total", [D, D])
        xp = sb("xp", [P, B + N])
        total = sb("total", [D, B])
        bias_row = sb("bias_row", [P, D])
        route = sb("route", [P, B, NP], I32)
        route_f = sb("route_f", [P, NP, B])
        route_x = sb("route_x", [P, N])
        mask_t = sb("mask_t", [NE, N])
        wi_raw = sb("wi_raw", [HID, D])
        wi_t = sb("wi_t", [D, HID])
        bi = vec_t[:, 0:1]
        wr_raw = sb("wr_raw", [HID, NL * NE, HID])
        wr_t = room[:, 0:8 * N].rearrange("p (e o) -> p e o", e=NL * NE)
        ws_raw = sb("ws_raw", [HID, NL, HID])
        ws_t = sb("ws_t", [HID, NL, HID])
        br = sb("br", [NE, NL, HID])
        bs = vec_t[:, 1:1 + NL]
        wo2_raw = sb("wo2_raw", [D, HID])
        wo2_t = sb("wo2_t", [HID, D])
        bo2_row = sb("bo2_row", [P, D])
        x4_t = room[0:D, 8 * N:9 * N]
        hf = early[:, 12 * N:15 * N].rearrange("p (l n) -> p l n", l=NL + 1)
        hm = early[:, 8 * N:12 * N].rearrange("p (u n) -> p u n", u=4)

        names = ("const grid wp posw1 posw2 bo wr w2e b1 b2 w1c w2c biasrow "
                 "route wi ws br wo2 bo2 out").split()
        dma = {n: sem("dma_" + n) for n in names}
        dma_x = [sem(f"dma_x{j}") for j in range(J)]
        dma_x2 = [sem(f"dma_x2_{j}") for j in range(J)]
        dma_qkvg = [sem(f"dma_qkvg{m}") for m in range(5)]
        dma_wod = [sem(f"dma_wod{m}") for m in range(4)]
        dma_w1 = [sem(f"dma_w1_{k}") for k in range(8)]
        dma_wr = [sem(f"dma_wr_{k}") for k in range(NL)]
        dma_pos = [sem(f"dma_pos{m}") for m in range(2)]
        dma_vec = sem("dma_vec")
        dma_w2h = sem("dma_w2h")
        dma_mw = [sem(f"dma_mw{m}") for m in range(3)]
        zeroed = sem("zeroed")
        pool_step = sem("pool_step")
        dve_step = sem("dve_step")
        act_step = sem("act_step")
        misc_turned = sem("misc_turned")
        misc_kept = sem("misc_kept")
        pos_made = sem("pos_made")
        pos_relu = sem("pos_relu")
        emb_made = sem("emb_made")
        emb_kept = sem("emb_kept")
        tok_made = sem("tok_made")
        var_ready = sem("var_ready")
        rstd_ready = sem("rstd_ready")
        x_norm = sem("x_norm")
        x1_turned = sem("x1_turned")
        mn_a = sem("mn_a")
        mn_b = sem("mn_b")
        proj_made = sem("proj_made")
        proj_act = sem("proj_act")
        proj_dve = sem("proj_dve")
        score_made = sem("score_made")
        vt_made = sem("vt_made")
        vt_act = sem("vt_act")
        vt_dve = sem("vt_dve")
        sm_bias_ready = sem("sm_bias_ready")
        sm_exp_ready = sem("sm_exp_ready")
        att_ready = sem("att_ready")
        att_turned = sem("att_turned")
        att_t_ready = sem("att_t_ready")
        o_made = sem("o_made")
        o_gated = sem("o_gated")
        wo_made = sem("wo_made")
        wo_act = sem("wo_act")
        wo_dve = sem("wo_dve")
        t2_made = sem("t2_made")
        x2_turned = sem("x2_turned")
        x2_kept = sem("x2_kept")
        x_split = sem("x_split")
        x_high = sem("x_high")
        wrt_made = sem("wrt_made")
        wrt_kept = sem("wrt_kept")
        ws_kept = sem("ws_kept")
        logit_made = sem("logit_made")
        gap_ready = sem("gap_ready")
        gap_exp_ready = sem("gap_exp_ready")
        comb_ready = sem("comb_ready")
        c_turned = sem("c_turned")
        c_kept = sem("c_kept")
        c_split = sem("c_split")
        w1_split = sem("w1_split")
        c_spread = sem("c_spread")
        h_made = sem("h_made")
        h_relu = sem("h_relu")
        h_gated = sem("h_gated")
        h_used = sem("h_used")
        moe_kept = sem("moe_kept")
        t3_made = sem("t3_made")
        x3_turned = sem("x3_turned")
        xp_top = sem("xp_top")
        xp_low = sem("xp_low")
        total_ready = sem("total_ready")
        wc_ready = sem("wc_ready")
        conv_made = sem("conv_made")
        conv_kept = sem("conv_kept")
        t4_made = sem("t4_made")
        x4_turned = sem("x4_turned")
        x4_kept = sem("x4_kept")
        mask_ready = sem("mask_ready")
        ffn_made = sem("ffn_made")
        ffn_relu = sem("ffn_relu")
        hm_ready = sem("hm_ready")
        hm_used = sem("hm_used")
        t5_made = sem("t5_made")
        h4_ready = sem("h4_ready")
        h_res = sem("h_res")
        h_resb = sem("h_resb")

        block = ctx.enter_context(nc.Block())

        img_src = I["x"].rearrange("b c (y q) w -> c q y b w", q=PATCH)
        row = lambda a: a.rearrange("(o n) -> o n", o=1)

        def load_image(eng, j, channels, done):
            for c in channels:
                for y in (2 * j, 2 * j + 1):
                    eng.dma_start(image[c * PATCH:(c + 1) * PATCH, y, :, :], img_src[c, :, y, :, :]).then_inc(done, 16)

        @block.sync
        def _(sp):
            sp.dma_start(wp[:, :, :], I["L0_tok_Wp"].rearrange("(k q) d -> k q d", q=PATCH)).then_inc(dma["wp"], 16)
            for j in range(J):
                load_image(sp, j, range(CH - 1), dma_x[j])
            for m, n in enumerate(("L0_attn_Wq", "L0_attn_Wk", "L0_attn_Wv", "L0_attn_Wg")):
                sp.dma_start(w_qkvg[0:D, m, :], I[n]).then_inc(dma_qkvg[m], 16)

            def load_w1(k):
                if k >= 4:
                    sp.wait_ge(w1_split, k - 3)
                for r in range(2):
                    sp.dma_start(w1_raw[r * D:(r + 1) * D, (k % 4) * 8:(k % 4 + 1) * 8, :],
                                 I["L0_ffn_W1"][8 * k:8 * k + 8].rearrange("e d h -> d e h")).then_inc(dma_w1[k], 16)

            for k in range(4):
                load_w1(k)
            for m in range(4):
                r = m % 2
                sp.wait_ge(zeroed, 1)
                sp.dma_start(wo_diag[m * HC:(m + 1) * HC, :, r * D:(r + 1) * D],
                             I["L0_attn_Wo"].rearrange("(h c) d -> c h d", c=HC)).then_inc(dma_wod[m], 16)
            sp.dma_start(w2e[:, :, :], I["L0_ffn_W2"].rearrange("e h d -> h e d")).then_inc(dma["w2e"], 16)
            for k in range(NL):
                sp.dma_start(wr_raw[:, k * NE:(k + 1) * NE, :],
                             I["L1_ffn_Wr"][k].rearrange("e o i -> o e i")).then_inc(dma_wr[k], 16)
            sp.dma_start(ws_raw[:, :, :], I["L1_ffn_Ws"].rearrange("l s o i -> o (l s) i")).then_inc(dma["ws"], 16)
            for k in range(4, 8):
                load_w1(k)
            sp.wait_ge(h4_ready, 1)
            dst = out.rearrange("b (j l) d -> j l b d", j=J)
            for j in range(J):
                sp.dma_start(dst[j], h4[:, j, :]).then_inc(dma["out"], 16)
            sp.wait_ge(dma["out"], 16 * J)

        @block.gpsimd
        def _(pool):
            steps = [0]

            def kept(ins):
                steps[0] += 1
                ins.then_inc(pool_step, 1)
                pool.wait_ge(pool_step, steps[0])

            filled = [0]

            def fill(tile, value):
                filled[0] += 1
                nc.gpsimd.memset(tile, value).then_inc(zeroed, 1)
                pool.wait_ge(zeroed, filled[0])

            fill(wo_diag[:, :, :], 0.0)
            fill(mw_rows[:, :], 0.0)
            fill(vec_rows[:, :], 0.0)
            fill(w_qkvg[D:D + 1, 0:3, :], 0.0)
            fill(mn_t[D:D + 1, :], 1.0)
            fill(x2_one[D:D + 1, :], 1.0)
            fill(pos_hid[D:D + 2, :], 1.0)
            fill(minus_half[:, :], -0.5)
            fill(xp[D:P, 0:B], 0.0)
            for j in range(J):
                load_image(pool, j, (CH - 1,), dma_x2[j])
            pool.dma_start(vec_rows[0:1, :], row(I["L1_ffn_bi"])).then_inc(dma_vec, 16)
            pool.dma_start(vec_rows[1:1 + NL, :], I["L1_ffn_bs"].rearrange("l s o -> (l s) o")).then_inc(dma_vec, 16)
            pool.dma_start(vec_rows[NL + 1:NL + 2, 0:D], row(I["L0_attn_gamma"])).then_inc(dma_vec, 16)
            pool.dma_start(vec_rows[NL + 2:NL + 3, 0:D], row(I["L0_attn_beta"])).then_inc(dma_vec, 16)
            mwsrc = I["L1_attn_memory_weights"]
            pool.dma_start(mw_rows[0:PAIRS - 1, :], mwsrc[0:TAPS, :].rearrange("(i k) d -> i (k d)", k=2)).then_inc(dma_mw[0], 16)
            pool.dma_start(mw_rows[PAIRS - 1:PAIRS, 0:D], mwsrc[TAPS:TAPS + 1, :]).then_inc(dma_mw[1], 16)
            for k in range(2):
                pool.dma_start(mw_rows[PAIRS:PAIRS + 1, k * D:(k + 1) * D], mwsrc[0:1, :]).then_inc(dma_mw[2], 16)
            pool.dma_start(b1_raw[:, :], I["L0_ffn_b1"]).then_inc(dma["b1"], 16)
            pool.dma_start(wi_raw[:, :], I["L1_ffn_Wi"]).then_inc(dma["wi"], 16)
            pool.dma_start(wo2_raw[:, :], I["L1_ffn_Wo"]).then_inc(dma["wo2"], 16)
            pool.dma_start(bo_row[:, :], row(I["L0_attn_bo"]).to_broadcast([P, D])).then_inc(dma["bo"], 16)
            pool.dma_start(bias_row[:, :], row(I["L1_attn_bias"]).to_broadcast([P, D])).then_inc(dma["biasrow"], 16)
            pool.dma_start(bo2_row[:, :], row(I["L1_ffn_bo"]).to_broadcast([P, D])).then_inc(dma["bo2"], 16)
            pool.dma_start(route[:, :, :].rearrange("p b y -> p (b y)"), row(I["L1_ffn_route_id"]).to_broadcast([P, T])).then_inc(dma["route"], 16)
            pool.dma_start(wr[0:D, :], I["L0_ffn_Wr"]).then_inc(dma["wr"], 16)
            pool.dma_start(wr[D:D + 1, :], row(I["L0_ffn_br"])).then_inc(dma["wr"], 16)
            pool.dma_start(b2e[:, :], I["L0_ffn_b2"]).then_inc(dma["b2"], 16)
            pool.dma_start(w2c[0:D, :], I["L1_attn_W2"]).then_inc(dma["w2c"], 16)
            pool.dma_start(w2c[D:P, :], I["L1_attn_W2"]).then_inc(dma_w2h, 16)
            pool.dma_start(br[:, :, :], I["L1_ffn_br"].rearrange("l e o -> e l o")).then_inc(dma["br"], 16)

            def inverse_root(n):
                pool.wait_ge(var_ready, n + 1)
                nc.gpsimd.tensor_tensor(rstd[:, :], var_arg[:, :], minus_half[:, :], ALU.pow).then_inc(rstd_ready, 1)
                pool.wait_ge(rstd_ready, n + 1)

            def with_bias(n, res, bias, load, dst):
                pool.wait_ge(dma[load], 16)
                pool.wait_ge(h_res, n + 1)
                nc.gpsimd.tensor_tensor(dst[:, :, :], res[:, :, :], bias[:, :].unsqueeze(1).to_broadcast([P, J, D]),
                                        ALU.add).then_inc(h_resb, 1)
                pool.wait_ge(h_resb, max(1, n))

            def split_w1(k):
                es = slice(k * E // 8, (k + 1) * E // 8)
                raw = slice((k % 4) * 8, (k % 4 + 1) * 8)
                pool.wait_ge(dma_w1[k], 32)
                kept(nc.gpsimd.tensor_scalar(w1_hl[:, es, :], w1_raw[:, raw, :], 1.0, 0.0, ALU.mult, ALU.add))
                nc.gpsimd.tensor_tensor(w1_hl[D:P, es, :], w1_raw[D:P, raw, :], w1_hl[D:P, es, :].bitcast(F32),
                                        ALU.subtract).then_inc(w1_split, 1)
                pool.wait_ge(w1_split, k + 1)

            inverse_root(0)
            with_bias(0, h0, bo_row, "bo", h0b)
            pool.wait_ge(misc_kept, 5)
            pool.wait_ge(dma["w2c"], 16)
            pool.wait_ge(dma_w2h, 16)
            kept(nc.gpsimd.tensor_tensor(mw_rel[:, :], mw_t[:, 0:PAIRS], mw_t[:, PAIRS:PAIRS + 1].to_broadcast([P, PAIRS]), ALU.subtract))
            kept(nc.gpsimd.tensor_tensor(wc[:, :, :], mw_rel[:, :].unsqueeze(2).to_broadcast([P, PAIRS, D]),
                                         w2c[:, :].unsqueeze(1).to_broadcast([P, PAIRS, D]), ALU.mult))
            nc.gpsimd.tensor_tensor(w_total[:, :], mw_t[0:D, PAIRS:PAIRS + 1].to_broadcast([D, D]), w2c[0:D, :],
                                    ALU.mult).then_inc(wc_ready, 1)
            pool.wait_ge(wc_ready, 1)
            pool.dma_start(wc[0:D, 0, :], I["L1_attn_W1"]).then_inc(dma["w1c"], 16)
            for k in range(8):
                split_w1(k)
            inverse_root(1)
            inverse_root(2)
            with_bias(2, h2, bias_row, "biasrow", h2b)
            inverse_root(3)
            with_bias(3, h3, bo2_row, "bo2", h3b)

        @block.scalar
        def _(act):
            A = nc.scalar.activation
            act.dma_start(const[:, :], I["const"]).then_inc(dma["const"], 16)
            act.dma_start(grid[:, :], I["grid"]).then_inc(dma["grid"], 16)
            act.dma_start(pos_w1[0:2, :], I["L0_tok_W1"]).then_inc(dma["posw1"], 16)
            act.dma_start(pos_w1[2:3, :], row(I["L0_tok_b1"])).then_inc(dma["posw1"], 16)
            act.dma_start(pos_w2[0:D, :], I["L0_tok_W2"]).then_inc(dma["posw2"], 16)
            act.dma_start(pos_w2[D:D + 1, :], row(I["L0_tok_b2"])).then_inc(dma_pos[0], 16)
            act.dma_start(pos_w2[D + 1:D + 2, :], row(I["L0_tok_bp"])).then_inc(dma_pos[1], 16)
            act.dma_start(w_qkvg[D:D + 1, 3, :], row(I["L0_attn_bg"])).then_inc(dma_qkvg[4], 16)

            act.wait_ge(pos_made, 1)
            A(pos_hid[0:D, :], bank[3][0:D, :], ACT.Relu).then_inc(pos_relu, 1)
            for j in range(J):
                act.wait_ge(emb_made, j + 1)
                A(emb_half[:, j * P:(j + 1) * P], bank[j % 2][:, 0:P], ACT.Copy).then_inc(emb_kept, 1)
            act.wait_ge(misc_kept, 5)
            act.wait_ge(x1_turned, 2)
            A(mn_t[0:D, N // 2:N], bank[5][0:D, 0:N // 2], ACT.Identity, bias=beta[:, 0:1], scale=gamma[:, 0:1]).then_inc(mn_b, 1)
            for m, dst in enumerate((q4, k4, v4)):
                act.wait_ge(proj_made, 2 * m + 1)
                A(dst[:, :, 0:4, :].rearrange("p l h b -> p h l b"), bank[2 * m][:, :].rearrange("p (h l b) -> p h l b", h=4, b=B),
                  ACT.Copy).then_inc(proj_act, 1)
            for k in range(2):
                act.wait_ge(proj_made, 7 + k)
                A(gexp[:, 4 * k:4 * k + 4, :, :].rearrange("p h l b -> p (h l b)"), bank[6 + k][:, :], ACT.Exp, scale=-1.0).then_inc(proj_act, 1)
            act.wait_ge(sm_bias_ready, 1)
            A(sm_exp[:, :], sm[:, :], ACT.Exp, bias=sm_bias[:, 0:1], scale=SCALE, accum_out=sm_sum[:, 0:1]).then_inc(sm_exp_ready, 1)
            for k in (0, 2):
                act.wait_ge(vt_made, k + 1)
                A(vt[:, 4 * k:4 * k + 4, :].rearrange("p l c -> p (l c)"), bank[1 + k][0:D, :], ACT.Copy).then_inc(vt_act, 1)
            act.wait_ge(wo_made, 1)
            A(wo_out[:, 0, :], bank[0][:, 0:P], ACT.Copy).then_inc(wo_act, 1)

            def keep_turned(g):
                act.wait_ge(wrt_made, g + 1)
                A(wr_t[:, 4 * g:4 * g + 4, :].rearrange("p e o -> p (e o)"), bank[5 + g % 2][:, :], ACT.Copy).then_inc(wrt_kept, 1)

            for g in range(4):
                keep_turned(g)
            act.wait_ge(x2_turned, 1)
            A(x2_t[:, :], bank[4][:, :], ACT.Copy).then_inc(x2_kept, 1)
            act.wait_ge(x2_kept, 1)
            A(x2_one[0:D, :], x2_t[0:D, :], ACT.Copy).then_inc(x2_kept, 1)
            A(x_ab[0:D, 0, :], x2_t[0:D, :], ACT.Copy).then_inc(x_high, 1)
            for g in range(4, NL * NE // 4):
                keep_turned(g)
            act.wait_ge(gap_ready, 1)
            A(gap_exp[:, :], gap[:, :], ACT.Exp).then_inc(gap_exp_ready, 1)
            act.wait_ge(c_turned, 1)
            A(c_t[:, :], bank[1][:, :], ACT.Copy).then_inc(c_kept, 1)
            act.wait_ge(c_kept, 1)
            A(c_hl[0:D, :], c_t[0:D, :], ACT.Copy).then_inc(c_split, 1)

            act.wait_ge(misc_kept, 5)

            def relu(e, u, first):
                act.wait_ge(h_made, e + 1)
                if not first:
                    act.wait_ge(h_gated, e - 3)
                A(hb[:, u, :], bank[(0, 2)[u % 2]][:, :], ACT.Relu, bias=b1_t[:, bass.ds(e, 1)]).then_inc(h_relu, 1)

            for u in range(4):
                relu(u, u, True)
            with act.Fori(1, E // 4) as g:
                for u in range(4):
                    relu(g * 4 + u, u, False)
            act.wait_ge(h_used, E // 2)
            A(half[:, :], bank[4][:, :], ACT.Copy).then_inc(moe_kept, 1)

            act.wait_ge(x3_turned, 1)
            A(xp[0:D, 0:N], bank[1][0:D, :], ACT.Copy).then_inc(xp_top, 1)
            act.wait_ge(conv_made, 1)
            A(half[:, :], bank[2][:, :], ACT.Copy).then_inc(conv_kept, 1)
            act.wait_ge(x4_turned, 1)
            A(x4_t[:, :], bank[5][0:D, :], ACT.Copy).then_inc(x4_kept, 1)
            act.wait_ge(ffn_made, 1)
            A(hf[:, 0, :], bank[6][:, :], ACT.Relu, bias=bi[:, 0:1]).then_inc(ffn_relu, 1)
            for l in range(NL):
                act.wait_ge(hm_used, (l + 1) * NE)
                A(hf[:, l + 1, :], bank[(7, 0)[l]][:, :], ACT.Relu, bias=bs[:, l:l + 1]).then_inc(ffn_relu, 1)

        @block.vector
        def _(dve):
            V = nc.vector
            steps = [0]

            def count(ins):
                steps[0] += 1
                ins.then_inc(dve_step, 1)

            def settle():
                dve.wait_ge(dve_step, steps[0])

            def kept(ins):
                count(ins)
                settle()

            def layer_norm(n, src, dst, scale, shift):
                for j in range(J):
                    count(V.bn_stats(stats[:, j, :], src[:, j, :]))
                settle()
                for j in range(J):
                    count(V.bn_aggr(mean_var[:, j, :], stats[:, j, :]))
                settle()
                V.tensor_scalar(var_arg[:, :], mean_var[:, :, 1], scale, shift, ALU.mult, ALU.add).then_inc(var_ready, 1)
                dve.wait_ge(rstd_ready, n + 1)
                for j in range(J):
                    for k in range(2 if n in (1, 2) else 1):
                        ins = V.tensor_scalar(dst[:, j, k, :], src[:, j, :], mean_var[:, j, 0:1], rstd[:, j:j + 1],
                                              ALU.subtract, ALU.mult)
                        if j < J - 1 or (k == 0 and n in (1, 2)):
                            count(ins)
                ins.then_inc(x_norm, 1)

            dve.wait_ge(misc_turned, 1)
            V.tensor_copy(wi_t[:, :], bank[6][0:D, 0:P]).then_inc(misc_kept, 1)
            V.tensor_copy(wo2_t[:, :], bank[6][:, 128:192]).then_inc(misc_kept, 1)
            V.tensor_copy(b1_t[:, :], bank[6][:, 192:256]).then_inc(misc_kept, 1)
            V.tensor_copy(mw_t[:, :], bank[6][:, 256:256 + PAIRS + 1]).then_inc(misc_kept, 1)
            V.tensor_copy(vec_t[:, :], bank[6][:, 280:280 + NL + 3]).then_inc(misc_kept, 1)
            dve.wait_ge(dma["route"], 16)
            kept(V.tensor_copy(route_f[:, :, :], route[:, :, :].rearrange("p b y -> p y b")))
            kept(V.tensor_copy(route_x[:, :].rearrange("p (y x b) -> p y x b", y=NP, b=B),
                               route_f[:, :, :].unsqueeze(2).to_broadcast([P, NP, NP, B])))
            dve.wait_ge(dma["const"], 16)
            V.tensor_scalar(mask_t[:, :], route_x[0:NE, :], part_no, None, ALU.is_equal).then_inc(mask_ready, 1)
            V.tensor_copy(fold_r[:, :], fold).then_inc(mask_ready, 1)

            dve.wait_ge(tok_made, 1)
            V.tensor_copy(h0[:, :, :], bank[2][:, 0:J * D].rearrange("p (j d) -> p j d", j=J)).then_inc(h_res, 1)
            dve.wait_ge(h_res, 1)
            layer_norm(0, h0, xn, 1.0 + EPS, EPS * EPS)
            dve.wait_ge(misc_kept, 5)
            dve.wait_ge(x1_turned, 1)
            V.tensor_scalar(mn_t[0:D, 0:N // 2], bank[4][0:D, 0:N // 2], gamma[:, 0:1], beta[:, 0:1], ALU.mult, ALU.add).then_inc(mn_a, 1)
            for m, dst in enumerate((q4, k4, v4)):
                dve.wait_ge(proj_made, 2 * m + 2)
                V.tensor_copy(dst[:, :, 4:8, :].rearrange("p l h b -> p h l b"),
                              bank[2 * m + 1][:, :].rearrange("p (h l b) -> p h l b", h=4, b=B)).then_inc(proj_dve, 1)
            dve.wait_ge(score_made, 1)
            kept(V.tensor_tensor(sm[:, :], bank[0][0:D, 0:D], off_head, ALU.add))
            kept(V.tensor_reduce(sm_max[:, :], sm[:, :], AX.X, ALU.max))
            V.tensor_scalar(sm_bias[:, :], sm_max[:, :], -SCALE, None, ALU.mult).then_inc(sm_bias_ready, 1)
            dve.wait_ge(proj_act, 5)
            kept(V.tensor_scalar(gexp[:, :, :, :], gexp[:, :, :, :], 1.0, None, ALU.add))
            dve.wait_ge(sm_exp_ready, 1)
            kept(V.reciprocal(sm_rec[:, :], sm_sum[:, :]))
            V.tensor_scalar(att[:, :], sm_exp[:, :], sm_rec[:, 0:1], None, ALU.mult).then_inc(att_ready, 1)
            for k in (1, 3):
                dve.wait_ge(vt_made, k + 1)
                V.tensor_copy(vt[:, 4 * k:4 * k + 4, :].rearrange("p l c -> p (l c)"), bank[1 + k][0:D, :]).then_inc(vt_dve, 1)
            dve.wait_ge(att_turned, 1)
            V.tensor_copy(att_t[:, :], bank[0][0:D, D:2 * D]).then_inc(att_t_ready, 1)
            kept(V.reciprocal(g4[:, :, :, :], gexp[:, :, :, :]))
            for k in range(2):
                dve.wait_ge(o_made, k + 1)
                ls = slice(8 * k, 8 * k + 8)
                V.tensor_tensor(o4[:, :, ls, :], bank[(7, 1)[k]][:, :].rearrange("p (l h b) -> p h l b", h=HEADS, b=B),
                                g4[:, :, ls, :], ALU.mult).then_inc(o_gated, 1)
            dve.wait_ge(wo_made, 2)
            V.tensor_copy(wo_out[:, 1, :], bank[2][:, 0:P]).then_inc(wo_dve, 1)
            dve.wait_ge(t2_made, 1)
            dve.wait_ge(h_resb, 1)
            V.tensor_tensor(h1[:, :, :], bank[3][:, 0:J * D].rearrange("p (j d) -> p j d", j=J), h0b[:, :, :], ALU.add).then_inc(h_res, 1)
            dve.wait_ge(h_res, 2)
            dve.wait_ge(x1_turned, 2)
            layer_norm(1, h1, xn, 1.0, EPS)

            dve.wait_ge(x2_kept, 1)
            kept(V.tensor_copy(x_ab[D:P, 1, :], x2_t[D:P, :]))
            V.tensor_tensor(x_ab[D:P, 0, :], x2_t[D:P, :], x_ab[D:P, 1, :].bitcast(F32), ALU.subtract).then_inc(x_split, 1)
            dve.wait_ge(x_high, 1)
            V.tensor_tensor(x_ab[0:D, 1, :], x2_t[0:D, :], x_ab[0:D, 0, :].bitcast(F32), ALU.subtract).then_inc(x_split, 1)
            dve.wait_ge(wrt_made, 9)
            V.tensor_tensor(ws_t[:, :, :], bank[5][:, 0:NL * P].rearrange("p (l o) -> p l o", l=NL),
                            ident.unsqueeze(1).to_broadcast([P, NL, P]), ALU.add).then_inc(ws_kept, 1)
            dve.wait_ge(logit_made, 1)
            kept(V.tensor_copy(logits[:, :, :], bank[7][:, 0:J * E].rearrange("p (j e) -> p j e", j=J)))
            for j in range(J):
                count(V.max(top8[:, j, :], logits[:, j, :]))
            settle()
            V.tensor_tensor(gap[:, :], top8[:, :, 1], top8[:, :, 0], ALU.subtract).then_inc(gap_ready, 1)
            for j in range(J):
                count(V.max_index(top_i[:, j, :], top8[:, j, :], logits[:, j, :]))
            settle()
            kept(V.tensor_copy(top_f[:, :, :], top_i[:, :, 0:2]))
            dve.wait_ge(gap_exp_ready, 1)
            kept(V.tensor_scalar(gate_sum[:, :], gap_exp[:, :], 1.0, None, ALU.add))
            kept(V.reciprocal(gate[:, 0, :], gate_sum[:, :]))
            kept(V.tensor_tensor(gate[:, 1, :], gate[:, 0, :], gap_exp[:, :], ALU.mult))
            for j in range(J):
                for k, dst in enumerate((comb1, comb2)):
                    count(V.tensor_scalar(dst[:, j, :], expert_no, top_f[:, j, k:k + 1], gate[:, k, j:j + 1], ALU.is_equal, ALU.mult))
            settle()
            for k in range(2):
                V.tensor_tensor(comb[:, :, k, :], comb1[:, :, :], comb2[:, :, :], ALU.add).then_inc(comb_ready, 1)
            dve.wait_ge(c_kept, 1)
            kept(V.tensor_copy(c_high[D:P, :], c_t[D:P, :]))
            V.tensor_tensor(c_hl[D:P, :], c_t[D:P, :], c_high[D:P, :].bitcast(F32), ALU.subtract).then_inc(x_split, 1)

            def gated(e, u, first):
                dve.wait_ge(h_relu, e + 1)
                dve.wait_ge(c_spread, e + 1)
                if not first:
                    dve.wait_ge(h_used, h_pair[u // 2])
                V.tensor_tensor(hg[:, u, :], bank[(3, 5, 6, 7)[u]][:, :], hb[:, u, :], ALU.mult).then_inc(h_gated, 1)

            for u in range(4):
                gated(u, u, True)
            with dve.Fori(1, E // 4) as g:
                h_pair = (g * 2 - 1, g * 2)
                for u in range(4):
                    gated(g * 4 + u, u, False)

            def residual(made, src_bank, before, dst, bias_count):
                dve.wait_ge(made, 1)
                if bias_count:
                    dve.wait_ge(h_resb, bias_count)
                V.tensor_tensor(dst[:, :, :], bank[src_bank][:, 0:J * D].rearrange("p (j d) -> p j d", j=J), before[:, :, :], ALU.add).then_inc(h_res, 1)

            residual(t3_made, 0, h1, h2, 0)
            dve.wait_ge(h_res, 3)
            layer_norm(2, h2, xn, 1.0, EPS)
            dve.wait_ge(x3_turned, 1)
            V.tensor_copy(xp[D:P, B:B + N], bank[1][D:P, :]).then_inc(xp_low, 1)
            dve.wait_ge(xp_top, 1)
            V.tensor_reduce(total[:, :], xp[0:D, 0:N].rearrange("p (t b) -> p b t", b=B), AX.X, ALU.add).then_inc(total_ready, 1)
            residual(t4_made, 3, h2b, h3, 2)
            dve.wait_ge(h_res, 4)
            layer_norm(3, h3, xn, 1.0, EPS)
            for l in range(NL):
                dve.wait_ge(ffn_relu, l + 1)
                for e in range(NE):
                    n = l * NE + e
                    if n >= 4:
                        dve.wait_ge(hm_used, n - 3)
                    V.scalar_tensor_tensor(hm[:, n % 4, :], route_x[:, :], float(e), hf[:, l, :], ALU.is_equal, ALU.mult).then_inc(hm_ready, 1)
            dve.wait_ge(t5_made, 1)
            dve.wait_ge(h_resb, 3)
            V.tensor_tensor(h4[:, :, :], bank[1][:, 0:J * D].rearrange("p (j d) -> p j d", j=J), h3b[:, :, :], ALU.add).then_inc(h4_ready, 1)

        @block.tensor
        def _(pe):
            mm = nc.tensor.matmul
            pe.wait_ge(dma["const"], 16)
            pe.wait_ge(dma["grid"], 16)
            pe.wait_ge(dma["posw1"], 32)
            mm(bank[3][0:D, :], pos_w1[:, :], grid[:, :], start=True, stop=True).then_inc(pos_made, 1)
            pe.wait_ge(dma["posw2"], 16)
            pe.wait_ge(dma_pos[0], 16)
            pe.wait_ge(dma_pos[1], 16)
            pe.wait_ge(dma["wp"], 16)
            pe.wait_ge(pos_relu, 1)
            pe.wait_ge(zeroed, 9)

            def embed(j):
                pe.wait_ge(dma_x[j], 64)
                pe.wait_ge(dma_x2[j], 32)
                if j >= 2:
                    pe.wait_ge(emb_kept, j - 1)
                px = image[:, 2 * j:2 * j + 2, :, :].rearrange("k y b (x q) -> k q y x b", q=PATCH)
                for q in range(PATCH):
                    r = q % 2
                    last = mm(bank[j % 2][r * D:(r + 1) * D, 0:P], wp[:, q, :], px[:, q, :, :, :], start=(q < 2), stop=(q >= PATCH - 2))
                last.then_inc(emb_made, 1)

            def embed_rows(j):
                pe.wait_ge(emb_kept, j + 1)
                dst = bank[2][:, j * D:(j + 1) * D]
                mm(dst, pos_hid[:, j * P:(j + 1) * P], pos_w2[:, :], start=True, stop=False)
                last = mm(dst, emb_half[:, j * P:(j + 1) * P], fold, start=False, stop=True)
                if j == J - 1:
                    last.then_inc(tok_made, 1)

            for j in range(J):
                embed(j)
                if j >= 1:
                    embed_rows(j - 1)
            embed_rows(J - 1)
            pe.wait_ge(dma["wi"], 16)
            nc.tensor.transpose(bank[6][0:D, 0:P], wi_raw[:, :], ident)
            pe.wait_ge(dma["wo2"], 16)
            nc.tensor.transpose(bank[6][:, 128:192], wo2_raw[:, :], ident[0:D, 0:D])
            pe.wait_ge(dma["b1"], 16)
            nc.tensor.transpose(bank[6][:, 192:256], b1_raw[:, :], ident[0:D, 0:D])
            pe.wait_ge(dma_mw[0], 16)
            pe.wait_ge(dma_mw[1], 16)
            pe.wait_ge(dma_mw[2], 32)
            nc.tensor.transpose(bank[6][:, 256:256 + PAIRS + 1], mw_rows[:, :], ident[0:PAIRS + 1, 0:PAIRS + 1])
            pe.wait_ge(dma_vec, 64)
            nc.tensor.transpose(bank[6][:, 280:280 + NL + 3], vec_rows[:, :], ident[0:NL + 3, 0:NL + 3]).then_inc(misc_turned, 1)

            pe.wait_ge(x_norm, 1)
            for j in range(J):
                last = nc.tensor.transpose(bank[4 + j // 2][0:D, (j % 2) * P:(j % 2 + 1) * P], xn[:, j, 0, :], ident)
                if j % 2:
                    last.then_inc(x1_turned, 1)
            for d in dma_qkvg:
                pe.wait_ge(d, 16)
            pe.wait_ge(mn_a, 1)
            pe.wait_ge(mn_b, 1)
            pe.wait_ge(misc_kept, 5)
            for m in range(4):
                for h in range(HEADS):
                    for j in range(J):
                        last = mm(bank[2 * m + h // 4][j * HC:(j + 1) * HC, (h % 4) * P:(h % 4 + 1) * P],
                                  w_qkvg[:, m, h * HC:(h + 1) * HC], mn_t[:, j * P:(j + 1) * P], start=True, stop=True,
                                  tile_position=(0, j * HC))
                    if h % 4 == 3:
                        last.then_inc(proj_made, 1)
            pe.wait_ge(proj_act, 2)
            pe.wait_ge(proj_dve, 2)
            for l in range(TJ):
                last = mm(bank[0][0:D, 0:D], q4[:, l, :, :].rearrange("p h b -> p (h b)"),
                          k4[:, l, :, :].rearrange("p h b -> p (h b)"), start=(l == 0), stop=(l == TJ - 1))
            last.then_inc(score_made, 1)
            pe.wait_ge(proj_act, 3)
            pe.wait_ge(proj_dve, 3)
            for l in range(TJ):
                last = nc.tensor.transpose(bank[1 + l // 4][0:D, (l % 4) * P:(l % 4 + 1) * P],
                                           v4[:, l, :, :].rearrange("p h b -> p (h b)"), ident)
                if l % 4 == 3:
                    last.then_inc(vt_made, 1)
            pe.wait_ge(att_ready, 1)
            nc.tensor.transpose(bank[0][0:D, D:2 * D], att[:, :], ident[0:D, 0:D]).then_inc(att_turned, 1)
            pe.wait_ge(att_t_ready, 1)
            pe.wait_ge(vt_act, 2)
            pe.wait_ge(vt_dve, 2)
            pe.wait_ge(proj_act, 5)
            for l in range(TJ):
                last = mm(bank[(7, 1)[l // 8]][:, (l % 8) * D:(l % 8 + 1) * D], vt[:, l, :], att_t[:, :], start=True, stop=True)
                if l % 8 == 7:
                    last.then_inc(o_made, 1)
            for d in dma_wod:
                pe.wait_ge(d, 16)
            pe.wait_ge(o_gated, 2)
            for q in range(2):
                rows = slice(q * D, (q + 1) * D)
                for h in range(HEADS):
                    last = mm(bank[(0, 2)[q]][:, 0:P], wo_diag[rows, h, :], o4[rows, h, :, :].rearrange("p l b -> p (l b)"),
                              start=(h == 0), stop=(h == HEADS - 1))
                last.then_inc(wo_made, 1)
            pe.wait_ge(wo_act, 1)
            nc.tensor.transpose(bank[3][:, 0:P], wo_out[:, 0, :], ident)
            pe.wait_ge(wo_dve, 1)
            nc.tensor.transpose(bank[3][:, P:2 * P], wo_out[:, 1, :], ident).then_inc(t2_made, 1)

            def turn_routed(g):
                if g >= 2:
                    pe.wait_ge(wrt_kept, g - 1)
                if g < 8:
                    pe.wait_ge(dma_wr[g // 4], 16)
                else:
                    pe.wait_ge(dma["ws"], 16)
                for k in range(4 if g < 8 else NL):
                    src = wr_raw[:, 4 * g + k, :] if g < 8 else ws_raw[:, k, :]
                    last = nc.tensor.transpose(bank[5 + g % 2][:, k * P:(k + 1) * P], src, ident)
                last.then_inc(wrt_made, 1)

            for g in range(4):
                turn_routed(g)
            pe.wait_ge(x_norm, 2)
            for j in range(J):
                last = nc.tensor.transpose(bank[4][:, j * P:(j + 1) * P], xn[:, j, :, :].rearrange("p k d -> p (k d)"), ident)
            last.then_inc(x2_turned, 1)
            for g in range(4, 9):
                turn_routed(g)
            pe.wait_ge(dma["wr"], 32)
            pe.wait_ge(x2_kept, 2)
            for j in range(J):
                last = mm(bank[7][:, j * E:(j + 1) * E], x2_one[:, j * P:(j + 1) * P], wr[:, :], start=True, stop=True)
            last.then_inc(logit_made, 1)
            pe.wait_ge(comb_ready, 2)
            for j in range(J):
                last = nc.tensor.transpose(bank[1][:, j * P:(j + 1) * P], comb[:, j, :, :].rearrange("p k e -> p (k e)"), ident)
            last.then_inc(c_turned, 1)
            pe.wait_ge(dma["b2"], 16)
            pe.wait_ge(c_kept, 1)
            mm(bank[4][0:D, :], b2e[:, :], c_t[0:D, :], start=True, stop=False)
            pe.wait_ge(c_split, 1)
            pe.wait_ge(x_split, 3)
            pe.wait_ge(wrt_kept, 8)
            pe.wait_ge(ws_kept, 1)
            pe.wait_ge(mask_ready, 2)
            pe.wait_ge(dma["w2e"], 16)

            def second_layer(i):
                pe.wait_ge(h_gated, 2 * i + 2)
                for k in range(2):
                    e = 2 * i + k
                    last = mm(bank[4][k * D:(k + 1) * D, :], w2e[:, e, :], hg[:, e % 4, :], start=(e == 1), stop=(e >= E - 2))
                last.then_inc(h_used, 1)

            for i in range(E // 2):
                for e in (2 * i, 2 * i + 1):
                    if e % 8 == 0:
                        pe.wait_ge(w1_split, e // 8 + 1)
                    if e >= 4:
                        pe.wait_ge(h_gated, e - 3)
                    mm(bank[(3, 5, 6, 7)[e % 4]][:, :], fold_r[:, e:e + 1].to_broadcast([P, P]), c_hl[:, :],
                       start=True, stop=True).then_inc(c_spread, 1)
                    if e >= 2:
                        pe.wait_ge(h_relu, e - 1)
                    mm(bank[(0, 2)[e % 2]][:, :], w1_hl[:, e, :], x_ab[:, 0, :], start=True, stop=False)
                    mm(bank[(0, 2)[e % 2]][:, :], w1_hl[:, e, :], x_ab[:, 1, :], start=False, stop=True).then_inc(h_made, 1)
                if i >= 1:
                    second_layer(i - 1)
            second_layer(E // 2 - 1)

            def fold_rows(dst, made):
                for j in range(J):
                    last = mm(bank[dst][:, j * D:(j + 1) * D], half[:, j * P:(j + 1) * P], fold, start=True, stop=True)
                last.then_inc(made, 1)

            pe.wait_ge(moe_kept, 1)
            fold_rows(0, t3_made)
            pe.wait_ge(x_norm, 3)
            for j in range(J):
                last = nc.tensor.transpose(bank[1][:, j * P:(j + 1) * P], xn[:, j, :, :].rearrange("p k d -> p (k d)"), ident)
            last.then_inc(x3_turned, 1)
            pe.wait_ge(wc_ready, 1)
            pe.wait_ge(dma["w1c"], 16)
            pe.wait_ge(xp_top, 1)
            pe.wait_ge(xp_low, 1)
            for i in range(PAIRS):
                r, lag = i % 2, 2 * i * B
                k = P if i < PAIRS - 1 else D
                if i == 1:
                    pe.wait_ge(total_ready, 1)
                    mm(bank[2][D:P, :].rearrange("p (t b) -> p t b", b=B), w_total[:, :],
                       total[:, :].unsqueeze(1).to_broadcast([D, T, B]), start=True, stop=False)
                last = mm(bank[2][r * D:(r + 1) * D, lag:N], wc[0:k, i, :], xp[0:k, 0:N - lag], start=(i == 0), stop=(i >= PAIRS - 2))
            last.then_inc(conv_made, 1)
            pe.wait_ge(conv_kept, 1)
            fold_rows(3, t4_made)
            pe.wait_ge(x_norm, 4)
            for j in range(J):
                last = nc.tensor.transpose(bank[5][0:D, j * P:(j + 1) * P], xn[:, j, 0, :], ident)
            last.then_inc(x4_turned, 1)
            pe.wait_ge(x4_kept, 1)
            mm(bank[6][:, :], wi_t[:, :], x4_t[:, :], start=True, stop=True).then_inc(ffn_made, 1)
            pe.wait_ge(dma["br"], 16)
            pe.wait_ge(mask_ready, 1)
            for l in range(NL):
                acc = bank[(7, 0)[l]][:, :]
                mm(acc, br[:, l, :], mask_t[:, :], start=True, stop=False)
                pe.wait_ge(ffn_relu, l + 1)
                mm(acc, ws_t[:, l, :], hf[:, l, :], start=False, stop=False)
                for e in range(NE):
                    n = l * NE + e
                    pe.wait_ge(hm_ready, n + 1)
                    last = mm(acc, wr_t[:, n, :], hm[:, n % 4, :], start=False, stop=(e == NE - 1))
                    last.then_inc(hm_used, 1)
            pe.wait_ge(ffn_relu, NL + 1)
            for j in range(J):
                last = mm(bank[1][:, j * D:(j + 1) * D], hf[:, NL, j * P:(j + 1) * P], wo2_t[:, :], start=True, stop=True)
            last.then_inc(t5_made, 1)


def constants():
    import numpy as np

    const = np.zeros((P, C_COLS), np.float32)
    const[:, C_ID:C_ID + P] = np.eye(P)
    const[:, C_II:C_II + D] = np.concatenate([np.eye(D)] * (P // D))
    const[:, C_IOTA:C_IOTA + E] = np.arange(E)
    head = np.arange(D) // B
    const[0:D, C_MASK:C_MASK + D] = np.where(head[:, None] == head[None, :], 0.0, -1e30)
    const[:, C_PART] = np.arange(P)
    t = np.arange(N) // B
    last = np.float32(NP - 1)
    grid = np.stack([(t // NP).astype(np.float32) / last, (t % NP).astype(np.float32) / last, np.ones(N, np.float32)])
    return {"const": const, "grid": grid}


def kernel(**inputs):
    import numpy as _np
    import concourse.bacc as _bacc
    from concourse import mybir as _mybir
    from concourse.bass_utils import run_bass_kernel_spmd as _run

    nc = _bacc.Bacc("TRN2", target_bir_lowering=False, num_devices=1)
    arrays, aps = {}, {}
    for name, a in {**inputs, **constants()}.items():
        a = _np.ascontiguousarray(a)
        arrays[f"in_{name}"] = a
        aps[name] = nc.dram_tensor(f"in_{name}", a.shape, _mybir.dt.from_np(a.dtype), kind="ExternalInput").ap()
    out = nc.dram_tensor("out", (B, T, D), F32, kind="ExternalOutput").ap()
    build_tower(nc, aps, out)
    r = _run(nc, [arrays], core_ids=[0])
    return r.results[0]["out"]
```

```python
from contextlib import ExitStack

import concourse.bass as bass
from concourse import mybir

F32 = mybir.dt.float32
F32R = mybir.dt.float32r
I32 = mybir.dt.int32
U32 = mybir.dt.uint32
ALU = mybir.AluOpType
ACT = mybir.ActivationFunctionType
AX = mybir.AxisListType

P = 128
B, CH, IMG, PATCH = 8, 3, 128, 16
NP = IMG // PATCH
T = NP * NP
N = B * T
J = N // P
TJ = T // J
D = 64
HEADS, HC = 8, 32
E, HID = 64, 128
TAPS = 40
PAIRS = TAPS // 2 + 1
NL, NE = 2, 16
EPS = 1e-5
SCALE = 1.0 / (HC ** 0.5) / (T ** 0.5)
KP = CH * PATCH

EARLY = dict(ident=(P, P), fold=(P, D), grid=(3, N), pos_w1=(3, D), pos_w2=(D + 2, D), gamma=(P, 1), beta=(P, 1),
             bg=(P, HEADS), expert_no=(P, E), off_head=(D, D), part_no=(P, 1), bo_row=(P, D))
LATE = dict(route=(P, T), wr=(D + 1, E), b1_t=(HID, E), b2e=(E, D), w2c=(P, D), mw_t=(P, PAIRS + 1), w1c=(D, D),
            bias_row=(P, D), wi_t=(D, HID), bi=(HID, 1), bs=(HID, NL), ws=(HID, NL * HID), br=(NE, NL * HID),
            wo2_t=(HID, D), bo2_row=(P, D))
KB = CH * PATCH * PATCH // P

def build_tower(nc, I, out):
    with ExitStack() as ctx:
        def sb(name, shape, dt=F32):
            return ctx.enter_context(nc.sbuf_tensor(name, shape, dt))

        def sem(name):
            return ctx.enter_context(nc.semaphore(name))

        bank = [ctx.enter_context(nc.psum_tensor(f"bank{i}", [P, 512], F32)) for i in range(8)]

        early = sb("early", [P, sum(c for _, c in EARLY.values())])
        late = sb("late", [P, sum(c for _, c in LATE.values())])

        def part(tile, table, name):
            at = 0
            for n, (rows, cols) in table.items():
                if n == name:
                    return tile[0:rows, at:at + cols]
                at += cols

        ident = part(early, EARLY, "ident")
        fold = part(early, EARLY, "fold")
        grid = part(early, EARLY, "grid")
        pos_w1 = part(early, EARLY, "pos_w1")
        pos_w2 = part(early, EARLY, "pos_w2")
        gamma = part(early, EARLY, "gamma")
        beta = part(early, EARLY, "beta")
        bg = part(early, EARLY, "bg")
        expert_no = part(early, EARLY, "expert_no")
        off_head = part(early, EARLY, "off_head")
        part_no = part(early, EARLY, "part_no")[0:NE]
        bo_row = part(early, EARLY, "bo_row")
        route = part(late, LATE, "route").bitcast(I32)
        wr = part(late, LATE, "wr")
        b1_t = part(late, LATE, "b1_t")
        b2e = part(late, LATE, "b2e")
        w2c = part(late, LATE, "w2c")
        mw_t = part(late, LATE, "mw_t")
        w1c = part(late, LATE, "w1c")
        bias_row = part(late, LATE, "bias_row")
        wi_t = part(late, LATE, "wi_t")
        bi = part(late, LATE, "bi")
        bs = part(late, LATE, "bs")
        ws = part(late, LATE, "ws")
        br = part(late, LATE, "br").rearrange("e (l o) -> e l o", l=NL)
        wo2_t = part(late, LATE, "wo2_t")
        bo2_row = part(late, LATE, "bo2_row")
        wide = sb("wide", [P, 8 * N])
        patches = wide[:, 0:KB * N].rearrange("p (k n) -> p k n", k=KB)
        wp = sb("wp", [P, KB, D])
        pos_hid = sb("pos_hid", [D + 2, N])
        room = sb("room", [P, 5 * TJ * D])
        emb_half = room[:, 9 * N:10 * N]
        h0 = sb("h0", [P, J, D])
        h0b = sb("h0b", [P, J, D])
        h1 = sb("h1", [P, J, D])
        h2 = sb("h2", [P, J, D])
        h2b = sb("h2b", [P, J, D])
        h3 = sb("h3", [P, J, D])
        h3b = sb("h3b", [P, J, D])
        h4 = sb("h4", [P, J, D])
        stats = sb("stats", [P, J, 6])
        mean_var = sb("mean_var", [P, J, 2])
        var_arg = sb("var_arg", [P, J])
        rstd = sb("rstd", [P, J])
        minus_half = sb("minus_half", [P, J])
        xn = sb("xn", [P, J, 2, D])
        mn_t = sb("mn_t", [P, 2, P])
        neg_bg = sb("neg_bg", [P, HEADS])
        w_qkvg = sb("w_qkvg", [P, 4, HEADS, D])
        q4 = room[:, 0 * N:2 * N].rearrange("p (l h b) -> p l h b", l=TJ, h=HEADS)
        k4 = room[:, 2 * N:4 * N].rearrange("p (l h b) -> p l h b", l=TJ, h=HEADS)
        v4 = room[:, 4 * N:6 * N].rearrange("p (l h b) -> p l h b", l=TJ, h=HEADS)
        gexp = sb("gexp", [P, HEADS, TJ, B])
        g4 = sb("g4", [P, HEADS, TJ, B])
        vt = room[0:D, 6 * N:10 * N].rearrange("p (l c) -> p l c", l=TJ)
        sm = sb("sm", [D, D])
        sm_max = sb("sm_max", [D, 1])
        sm_bias = sb("sm_bias", [D, 1])
        sm_exp = sb("sm_exp", [D, D])
        sm_sum = sb("sm_sum", [D, 1])
        sm_rec = sb("sm_rec", [D, 1])
        att = sb("att", [D, D])
        att_t = sb("att_t", [D, D])
        o4 = gexp
        wo_diag = sb("wo_diag", [P, HEADS, P])
        wo_out = sb("wo_out", [P, 2, P])
        x2_t = room[:, 8 * N:9 * N]
        x2_one = sb("x2_one", [D + 1, N])
        x_ab = sb("x_ab", [P, 2, N], F32R)
        w1_raw = sb("w1_raw", [P, E // 2, HID])
        w1_hl = sb("w1_hl", [P, E, HID], F32R)
        w2e = sb("w2e", [HID, E, D])
        logits = sb("logits", [P, J, E])
        top8 = sb("top8", [P, J, 8])
        top_i = sb("top_i", [P, J, 8], U32)
        top_f = sb("top_f", [P, J, 2])
        gap = sb("gap", [P, J])
        gap_exp = sb("gap_exp", [P, J])
        gate_sum = sb("gate_sum", [P, J])
        gate = sb("gate", [P, 2, J])
        comb1 = sb("comb1", [P, J, E])
        comb2 = sb("comb2", [P, J, E])
        comb = sb("comb", [P, J, 2, E])
        c_t = room[:, 9 * N:10 * N]
        c_high = sb("c_high", [P, N], F32R)
        c_hl = sb("c_hl", [P, N], F32R)
        fold_r = sb("fold_r", [P, D], F32R)
        hb = wide[:, 0:4 * N].rearrange("p (u n) -> p u n", u=4)
        hg = wide[:, 4 * N:8 * N].rearrange("p (u n) -> p u n", u=4)
        half = sb("half", [P, N])
        mw_rel = sb("mw_rel", [P, PAIRS])
        wc = sb("wc", [P, PAIRS, D])
        w_total = sb("w_total", [D, D])
        xp = sb("xp", [P, B + N])
        total = sb("total", [D, B])
        route_f = sb("route_f", [P, NP, B])
        route_x = sb("route_x", [P, N])
        mask_t = sb("mask_t", [NE, N])
        wr_t = sb("wr_t", [HID, NL * NE, HID])
        ws_t = sb("ws_t", [HID, NL, HID])
        x4_t = room[0:D, 8 * N:9 * N]
        hf = wide[:, 4 * N:7 * N].rearrange("p (l n) -> p l n", l=NL + 1)
        hm = wide[:, 0:4 * N].rearrange("p (u n) -> p u n", u=4)

        dma = {n: sem("dma_" + n) for n in ("early", "late", "wp", "qkvg", "wo", "w2e", "wr_t", "out")}
        dma_x = [sem(f"dma_x{k}") for k in range(KB // 2)]
        dma_w1 = [sem(f"dma_w1_{k}") for k in range(8)]
        zeroed = sem("zeroed")
        pool_step = sem("pool_step")
        dve_step = sem("dve_step")
        act_step = sem("act_step")
        pos_made = sem("pos_made")
        pos_relu = sem("pos_relu")
        emb_made = sem("emb_made")
        emb_kept = sem("emb_kept")
        tok_made = sem("tok_made")
        var_ready = sem("var_ready")
        rstd_ready = sem("rstd_ready")
        x_norm = sem("x_norm")
        x1_turned = sem("x1_turned")
        mn_a = sem("mn_a")
        mn_b = sem("mn_b")
        proj_made = sem("proj_made")
        proj_act = sem("proj_act")
        proj_dve = sem("proj_dve")
        score_made = sem("score_made")
        vt_made = sem("vt_made")
        vt_act = sem("vt_act")
        vt_dve = sem("vt_dve")
        sm_bias_ready = sem("sm_bias_ready")
        sm_exp_ready = sem("sm_exp_ready")
        att_ready = sem("att_ready")
        att_turned = sem("att_turned")
        att_t_ready = sem("att_t_ready")
        o_made = sem("o_made")
        o_gated = sem("o_gated")
        wo_made = sem("wo_made")
        wo_act = sem("wo_act")
        wo_dve = sem("wo_dve")
        t2_made = sem("t2_made")
        x2_turned = sem("x2_turned")
        x2_kept = sem("x2_kept")
        x_split = sem("x_split")
        x_high = sem("x_high")
        ws_kept = sem("ws_kept")
        fold_ready = sem("fold_ready")
        logit_made = sem("logit_made")
        gap_ready = sem("gap_ready")
        gap_exp_ready = sem("gap_exp_ready")
        comb_ready = sem("comb_ready")
        c_turned = sem("c_turned")
        c_kept = sem("c_kept")
        c_split = sem("c_split")
        w1_split = sem("w1_split")
        c_spread = sem("c_spread")
        h_made = sem("h_made")
        h_relu = sem("h_relu")
        h_gated = sem("h_gated")
        h_used = sem("h_used")
        moe_kept = sem("moe_kept")
        t3_made = sem("t3_made")
        x3_turned = sem("x3_turned")
        xp_top = sem("xp_top")
        xp_low = sem("xp_low")
        total_ready = sem("total_ready")
        wc_ready = sem("wc_ready")
        conv_made = sem("conv_made")
        conv_kept = sem("conv_kept")
        t4_made = sem("t4_made")
        x4_turned = sem("x4_turned")
        x4_kept = sem("x4_kept")
        mask_ready = sem("mask_ready")
        ffn_made = sem("ffn_made")
        ffn_relu = sem("ffn_relu")
        hm_ready = sem("hm_ready")
        hm_used = sem("hm_used")
        t5_made = sem("t5_made")
        h4_ready = sem("h4_ready")
        h_res = sem("h_res")
        h_resb = sem("h_resb")

        block = ctx.enter_context(nc.Block())

        @block.sync
        def _(sp):
            sp.dma_start(wp[:, :, :], I["wp"]).then_inc(dma["wp"], 16)
            for k in range(KB // 2):
                sp.dma_start(patches[:, 2 * k:2 * k + 2, :], I["patches"][:, 2 * k:2 * k + 2, :]).then_inc(dma_x[k], 16)
            sp.dma_start(w_qkvg[:, :, :, :], I["qkvg"]).then_inc(dma["qkvg"], 16)

            def load_w1(k):
                if k >= 4:
                    sp.wait_ge(w1_split, k - 3)
                for r in range(2):
                    sp.dma_start(w1_raw[r * D:(r + 1) * D, (k % 4) * 8:(k % 4 + 1) * 8, :],
                                 I["w1"][:, 8 * k:8 * k + 8, :]).then_inc(dma_w1[k], 16)

            for k in range(4):
                load_w1(k)
            sp.dma_start(wo_diag[:, :, :], I["wo_diag"]).then_inc(dma["wo"], 16)
            sp.dma_start(late[:, :], I["late"]).then_inc(dma["late"], 16)
            sp.dma_start(w2e[:, :, :], I["w2e"]).then_inc(dma["w2e"], 16)
            for k in range(4, 8):
                load_w1(k)
            sp.dma_start(wr_t[:, :, :], I["wr_t"]).then_inc(dma["wr_t"], 16)
            sp.wait_ge(h4_ready, 1)
            sp.dma_start(out, h4[:, :, :]).then_inc(dma["out"], 16)
            sp.wait_ge(dma["out"], 16)

        @block.gpsimd
        def _(pool):
            steps = [0]

            def kept(ins):
                steps[0] += 1
                ins.then_inc(pool_step, 1)
                pool.wait_ge(pool_step, steps[0])

            filled = [0]

            def fill(tile, value):
                filled[0] += 1
                nc.gpsimd.memset(tile, value).then_inc(zeroed, 1)
                pool.wait_ge(zeroed, filled[0])

            fill(pos_hid[D:D + 2, :], 1.0)
            fill(minus_half[:, :], -0.5)
            fill(x2_one[D:D + 1, :], 1.0)
            fill(xp[D:P, 0:B], 0.0)

            def inverse_root(n):
                pool.wait_ge(var_ready, n + 1)
                nc.gpsimd.tensor_tensor(rstd[:, :], var_arg[:, :], minus_half[:, :], ALU.pow).then_inc(rstd_ready, 1)
                pool.wait_ge(rstd_ready, n + 1)

            def with_bias(n, res, bias, load, dst):
                pool.wait_ge(load, 16)
                pool.wait_ge(h_res, n + 1)
                nc.gpsimd.tensor_tensor(dst[:, :, :], res[:, :, :], bias[:, :].unsqueeze(1).to_broadcast([P, J, D]),
                                        ALU.add).then_inc(h_resb, 1)
                pool.wait_ge(h_resb, max(1, n))

            def split_w1(k):
                es = slice(k * E // 8, (k + 1) * E // 8)
                raw = slice((k % 4) * 8, (k % 4 + 1) * 8)
                pool.wait_ge(dma_w1[k], 32)
                kept(nc.gpsimd.tensor_scalar(w1_hl[:, es, :], w1_raw[:, raw, :], 1.0, 0.0, ALU.mult, ALU.add))
                nc.gpsimd.tensor_tensor(w1_hl[D:P, es, :], w1_raw[D:P, raw, :], w1_hl[D:P, es, :].bitcast(F32),
                                        ALU.subtract).then_inc(w1_split, 1)
                pool.wait_ge(w1_split, k + 1)

            inverse_root(0)
            with_bias(0, h0, bo_row, dma["early"], h0b)
            pool.wait_ge(dma["late"], 16)
            kept(nc.gpsimd.tensor_tensor(mw_rel[:, :], mw_t[:, 0:PAIRS], mw_t[:, PAIRS:PAIRS + 1].to_broadcast([P, PAIRS]), ALU.subtract))
            kept(nc.gpsimd.tensor_tensor(wc[:, :, :], mw_rel[:, :].unsqueeze(2).to_broadcast([P, PAIRS, D]),
                                         w2c.unsqueeze(1).to_broadcast([P, PAIRS, D]), ALU.mult))
            kept(nc.gpsimd.tensor_copy(wc[0:D, 0, :], w1c))
            nc.gpsimd.tensor_tensor(w_total[:, :], mw_t[0:D, PAIRS:PAIRS + 1].to_broadcast([D, D]), w2c[0:D],
                                    ALU.mult).then_inc(wc_ready, 1)
            pool.wait_ge(wc_ready, 1)
            for k in range(8):
                split_w1(k)
            inverse_root(1)
            inverse_root(2)
            with_bias(2, h2, bias_row, dma["late"], h2b)
            inverse_root(3)
            with_bias(3, h3, bo2_row, dma["late"], h3b)

        @block.scalar
        def _(act):
            A = nc.scalar.activation
            act.dma_start(early[:, :], I["early"]).then_inc(dma["early"], 16)

            act.wait_ge(pos_made, 1)
            A(pos_hid[0:D, :], bank[3][0:D, :], ACT.Relu).then_inc(pos_relu, 1)
            act.wait_ge(emb_made, 1)
            A(emb_half[:, :], bank[0][:, :], ACT.Copy).then_inc(emb_kept, 1)
            act.wait_ge(x1_turned, 1)
            A(mn_t[:, :, :].rearrange("p q n -> p (q n)"), bank[4][:, 0:2 * P], ACT.Identity, bias=beta, scale=gamma).then_inc(mn_a, 1)
            for m, dst in enumerate((q4, k4, v4)):
                act.wait_ge(proj_made, 2 * m + 1)
                A(dst[:, :, 0:4, :].rearrange("p l h b -> p h l b"), bank[2 * m][:, :].rearrange("p (h l b) -> p h l b", h=4, b=B),
                  ACT.Copy).then_inc(proj_act, 1)
            act.wait_ge(x_norm, 1)
            for h in range(HEADS):
                act.wait_ge(proj_made, 7 + h // 4)
                A(gexp[:, h, :, :].rearrange("p l b -> p (l b)"), bank[6 + h // 4][:, (h % 4) * P:(h % 4 + 1) * P], ACT.Exp,
                  bias=neg_bg[:, h:h + 1], scale=-1.0).then_inc(proj_act, 1)
            act.wait_ge(sm_bias_ready, 1)
            A(sm_exp[:, :], sm[:, :], ACT.Exp, bias=sm_bias[:, 0:1], scale=SCALE, accum_out=sm_sum[:, 0:1]).then_inc(sm_exp_ready, 1)
            for k in (0, 2):
                act.wait_ge(vt_made, k + 1)
                A(vt[:, 4 * k:4 * k + 4, :].rearrange("p l c -> p (l c)"), bank[1 + k][0:D, :], ACT.Copy).then_inc(vt_act, 1)
            act.wait_ge(wo_made, 1)
            A(wo_out[:, 0, :], bank[0][:, 0:P], ACT.Copy).then_inc(wo_act, 1)

            act.wait_ge(x2_turned, 1)
            A(x2_t[:, :], bank[4][:, :], ACT.Copy).then_inc(x2_kept, 1)
            act.wait_ge(x2_kept, 1)
            A(x2_one[0:D, :], x2_t[0:D, :], ACT.Copy).then_inc(x2_kept, 1)
            A(x_ab[0:D, 0, :], x2_t[0:D, :], ACT.Copy).then_inc(x_high, 1)
            act.wait_ge(gap_ready, 1)
            A(gap_exp[:, :], gap[:, :], ACT.Exp).then_inc(gap_exp_ready, 1)
            act.wait_ge(c_turned, 1)
            A(c_t[:, :], bank[1][:, :], ACT.Copy).then_inc(c_kept, 1)
            act.wait_ge(c_kept, 1)
            A(c_hl[0:D, :], c_t[0:D, :], ACT.Copy).then_inc(c_split, 1)

            act.wait_ge(dma["late"], 16)

            def relu(e, u, first):
                act.wait_ge(h_made, e + 1)
                if not first:
                    act.wait_ge(h_gated, e - 3)
                A(hb[:, u, :], bank[(0, 2)[u % 2]][:, :], ACT.Relu, bias=b1_t[:, bass.ds(e, 1)]).then_inc(h_relu, 1)

            for u in range(4):
                relu(u, u, True)
            with act.Fori(1, E // 4) as g:
                for u in range(4):
                    relu(g * 4 + u, u, False)
            act.wait_ge(h_used, E // 2)
            A(half[:, :], bank[4][:, :], ACT.Copy).then_inc(moe_kept, 1)

            act.wait_ge(x3_turned, 1)
            A(xp[0:D, 0:N], bank[1][0:D, :], ACT.Copy).then_inc(xp_top, 1)
            act.wait_ge(conv_made, 1)
            A(half[:, :], bank[2][:, :], ACT.Copy).then_inc(conv_kept, 1)
            act.wait_ge(x4_turned, 1)
            A(x4_t[:, :], bank[5][0:D, :], ACT.Copy).then_inc(x4_kept, 1)
            act.wait_ge(ffn_made, 1)
            A(hf[:, 0, :], bank[6][:, :], ACT.Relu, bias=bi[:, 0:1]).then_inc(ffn_relu, 1)
            for l in range(NL):
                act.wait_ge(hm_used, (l + 1) * NE)
                A(hf[:, l + 1, :], bank[(7, 0)[l]][:, :], ACT.Relu, bias=bs[:, l:l + 1]).then_inc(ffn_relu, 1)

        @block.vector
        def _(dve):
            V = nc.vector
            steps = [0]

            def count(ins):
                steps[0] += 1
                ins.then_inc(dve_step, 1)

            def settle():
                dve.wait_ge(dve_step, steps[0])

            def kept(ins):
                count(ins)
                settle()

            def layer_norm(n, src, dst, scale, shift):
                for j in range(J):
                    count(V.bn_stats(stats[:, j, :], src[:, j, :]))
                settle()
                for j in range(J):
                    count(V.bn_aggr(mean_var[:, j, :], stats[:, j, :]))
                settle()
                V.tensor_scalar(var_arg[:, :], mean_var[:, :, 1], scale, shift, ALU.mult, ALU.add).then_inc(var_ready, 1)
                dve.wait_ge(rstd_ready, n + 1)
                for j in range(J):
                    for k in range(2 if n in (1, 2) else 1):
                        ins = V.tensor_scalar(dst[:, j, k, :] if n else dst[:, j // 2, j % 2, :], src[:, j, :], mean_var[:, j, 0:1], rstd[:, j:j + 1],
                                              ALU.subtract, ALU.mult)
                        if j < J - 1 or (k == 0 and n in (1, 2)):
                            count(ins)
                ins.then_inc(x_norm, 1)

            dve.wait_ge(dma["early"], 16)
            kept(V.tensor_scalar(neg_bg[:, :], bg, -1.0, None, ALU.mult))
            V.tensor_copy(fold_r[:, :], fold).then_inc(fold_ready, 1)

            dve.wait_ge(tok_made, 1)
            V.tensor_copy(h0[:, :, :], bank[2][:, 0:J * D].rearrange("p (j d) -> p j d", j=J)).then_inc(h_res, 1)
            dve.wait_ge(h_res, 1)
            layer_norm(0, h0, xn, 1.0 + EPS, EPS * EPS)
            dve.wait_ge(dma["late"], 16)
            kept(V.tensor_copy(route_f[:, :, :], route.rearrange("p (b y) -> p y b", b=B)))
            kept(V.tensor_copy(route_x[:, :].rearrange("p (y x b) -> p y x b", y=NP, b=B),
                               route_f[:, :, :].unsqueeze(2).to_broadcast([P, NP, NP, B])))
            V.tensor_scalar(mask_t[:, :], route_x[0:NE, :], part_no, None, ALU.is_equal).then_inc(mask_ready, 1)
            V.tensor_tensor(ws_t[:, :, :], ws.rearrange("p (l o) -> p l o", l=NL), ident.unsqueeze(1).to_broadcast([P, NL, P]),
                            ALU.add).then_inc(ws_kept, 1)
            for m, dst in enumerate((q4, k4, v4)):
                dve.wait_ge(proj_made, 2 * m + 2)
                V.tensor_copy(dst[:, :, 4:8, :].rearrange("p l h b -> p h l b"),
                              bank[2 * m + 1][:, :].rearrange("p (h l b) -> p h l b", h=4, b=B)).then_inc(proj_dve, 1)
            dve.wait_ge(score_made, 1)
            kept(V.tensor_tensor(sm[:, :], bank[0][0:D, 0:D], off_head, ALU.add))
            kept(V.tensor_reduce(sm_max[:, :], sm[:, :], AX.X, ALU.max))
            V.tensor_scalar(sm_bias[:, :], sm_max[:, :], -SCALE, None, ALU.mult).then_inc(sm_bias_ready, 1)
            dve.wait_ge(proj_act, 3 + HEADS)
            kept(V.tensor_scalar(gexp[:, :, :, :], gexp[:, :, :, :], 1.0, None, ALU.add))
            dve.wait_ge(sm_exp_ready, 1)
            kept(V.reciprocal(sm_rec[:, :], sm_sum[:, :]))
            V.tensor_scalar(att[:, :], sm_exp[:, :], sm_rec[:, 0:1], None, ALU.mult).then_inc(att_ready, 1)
            for k in (1, 3):
                dve.wait_ge(vt_made, k + 1)
                V.tensor_copy(vt[:, 4 * k:4 * k + 4, :].rearrange("p l c -> p (l c)"), bank[1 + k][0:D, :]).then_inc(vt_dve, 1)
            dve.wait_ge(att_turned, 1)
            V.tensor_copy(att_t[:, :], bank[0][0:D, D:2 * D]).then_inc(att_t_ready, 1)
            kept(V.reciprocal(g4[:, :, :, :], gexp[:, :, :, :]))
            for k in range(2):
                dve.wait_ge(o_made, k + 1)
                ls = slice(8 * k, 8 * k + 8)
                V.tensor_tensor(o4[:, :, ls, :], bank[(7, 1)[k]][:, :].rearrange("p (l h b) -> p h l b", h=HEADS, b=B),
                                g4[:, :, ls, :], ALU.mult).then_inc(o_gated, 1)
            dve.wait_ge(wo_made, 2)
            V.tensor_copy(wo_out[:, 1, :], bank[2][:, 0:P]).then_inc(wo_dve, 1)
            dve.wait_ge(t2_made, 1)
            dve.wait_ge(h_resb, 1)
            V.tensor_tensor(h1[:, :, :], bank[3][:, 0:J * D].rearrange("p (j d) -> p j d", j=J), h0b[:, :, :], ALU.add).then_inc(h_res, 1)
            dve.wait_ge(h_res, 2)
            dve.wait_ge(x1_turned, 1)
            layer_norm(1, h1, xn, 1.0, EPS)

            dve.wait_ge(x2_kept, 1)
            kept(V.tensor_copy(x_ab[D:P, 1, :], x2_t[D:P, :]))
            V.tensor_tensor(x_ab[D:P, 0, :], x2_t[D:P, :], x_ab[D:P, 1, :].bitcast(F32), ALU.subtract).then_inc(x_split, 1)
            dve.wait_ge(x_high, 1)
            V.tensor_tensor(x_ab[0:D, 1, :], x2_t[0:D, :], x_ab[0:D, 0, :].bitcast(F32), ALU.subtract).then_inc(x_split, 1)
            dve.wait_ge(logit_made, 1)
            kept(V.tensor_copy(logits[:, :, :], bank[7][:, 0:J * E].rearrange("p (j e) -> p j e", j=J)))
            for j in range(J):
                count(V.max(top8[:, j, :], logits[:, j, :]))
            settle()
            V.tensor_tensor(gap[:, :], top8[:, :, 1], top8[:, :, 0], ALU.subtract).then_inc(gap_ready, 1)
            for j in range(J):
                count(V.max_index(top_i[:, j, :], top8[:, j, :], logits[:, j, :]))
            settle()
            kept(V.tensor_copy(top_f[:, :, :], top_i[:, :, 0:2]))
            dve.wait_ge(gap_exp_ready, 1)
            kept(V.tensor_scalar(gate_sum[:, :], gap_exp[:, :], 1.0, None, ALU.add))
            kept(V.reciprocal(gate[:, 0, :], gate_sum[:, :]))
            kept(V.tensor_tensor(gate[:, 1, :], gate[:, 0, :], gap_exp[:, :], ALU.mult))
            for j in range(J):
                for k, dst in enumerate((comb1, comb2)):
                    count(V.tensor_scalar(dst[:, j, :], expert_no, top_f[:, j, k:k + 1], gate[:, k, j:j + 1], ALU.is_equal, ALU.mult))
            settle()
            for k in range(2):
                V.tensor_tensor(comb[:, :, k, :], comb1[:, :, :], comb2[:, :, :], ALU.add).then_inc(comb_ready, 1)
            dve.wait_ge(c_kept, 1)
            kept(V.tensor_copy(c_high[D:P, :], c_t[D:P, :]))
            V.tensor_tensor(c_hl[D:P, :], c_t[D:P, :], c_high[D:P, :].bitcast(F32), ALU.subtract).then_inc(x_split, 1)

            def gated(e, u, first):
                dve.wait_ge(h_relu, e + 1)
                dve.wait_ge(c_spread, e + 1)
                if not first:
                    dve.wait_ge(h_used, h_pair[u // 2])
                V.tensor_tensor(hg[:, u, :], bank[(3, 5, 6, 7)[u]][:, :], hb[:, u, :], ALU.mult).then_inc(h_gated, 1)

            for u in range(4):
                gated(u, u, True)
            with dve.Fori(1, E // 4) as g:
                h_pair = (g * 2 - 1, g * 2)
                for u in range(4):
                    gated(g * 4 + u, u, False)

            def residual(made, src_bank, before, dst, bias_count):
                dve.wait_ge(made, 1)
                if bias_count:
                    dve.wait_ge(h_resb, bias_count)
                V.tensor_tensor(dst[:, :, :], bank[src_bank][:, 0:J * D].rearrange("p (j d) -> p j d", j=J), before[:, :, :], ALU.add).then_inc(h_res, 1)

            residual(t3_made, 0, h1, h2, 0)
            dve.wait_ge(h_res, 3)
            layer_norm(2, h2, xn, 1.0, EPS)
            dve.wait_ge(x3_turned, 1)
            V.tensor_copy(xp[D:P, B:B + N], bank[1][D:P, :]).then_inc(xp_low, 1)
            dve.wait_ge(xp_top, 1)
            V.tensor_reduce(total[:, :], xp[0:D, 0:N].rearrange("p (t b) -> p b t", b=B), AX.X, ALU.add).then_inc(total_ready, 1)
            residual(t4_made, 3, h2b, h3, 2)
            dve.wait_ge(h_res, 4)
            layer_norm(3, h3, xn, 1.0, EPS)
            for l in range(NL):
                dve.wait_ge(ffn_relu, l + 1)
                for e in range(NE):
                    n = l * NE + e
                    if n >= 4:
                        dve.wait_ge(hm_used, n - 3)
                    V.scalar_tensor_tensor(hm[:, n % 4, :], route_x[:, :], float(e), hf[:, l, :], ALU.is_equal, ALU.mult).then_inc(hm_ready, 1)
            dve.wait_ge(t5_made, 1)
            dve.wait_ge(h_resb, 3)
            V.tensor_tensor(h4[:, :, :], bank[1][:, 0:J * D].rearrange("p (j d) -> p j d", j=J), h3b[:, :, :], ALU.add).then_inc(h4_ready, 1)

        @block.tensor
        def _(pe):
            mm = nc.tensor.matmul
            pe.wait_ge(dma["early"], 16)
            mm(bank[3][0:D, :], pos_w1, grid, start=True, stop=True).then_inc(pos_made, 1)
            pe.wait_ge(dma["wp"], 16)
            for k in range(KB):
                if k % 2 == 0:
                    pe.wait_ge(dma_x[k // 2], 16)
                r = k % 2
                last = mm(bank[0][r * D:(r + 1) * D, :], wp[:, k, :], patches[:, k, :], start=(k < 2), stop=(k >= KB - 2))
            last.then_inc(emb_made, 1)
            pe.wait_ge(pos_relu, 1)
            pe.wait_ge(zeroed, 1)
            pe.wait_ge(emb_kept, 1)
            for j in range(J):
                dst = bank[2][:, j * D:(j + 1) * D]
                mm(dst, pos_hid[:, j * P:(j + 1) * P], pos_w2, start=True, stop=False)
                last = mm(dst, emb_half[:, j * P:(j + 1) * P], fold, start=False, stop=True)
            last.then_inc(tok_made, 1)

            pe.wait_ge(x_norm, 1)
            for q in range(2):
                last = nc.tensor.transpose(bank[4][:, q * P:(q + 1) * P], xn[:, q, :, :].rearrange("p r d -> p (r d)"), ident)
            last.then_inc(x1_turned, 1)
            pe.wait_ge(dma["qkvg"], 16)
            pe.wait_ge(mn_a, 1)
            for m in range(4):
                for h in range(HEADS):
                    for q in range(2):
                        last = mm(bank[2 * m + h // 4][q * D:(q + 1) * D, (h % 4) * P:(h % 4 + 1) * P],
                                  w_qkvg[:, m, h, :], mn_t[:, q, :], start=True, stop=True)
                    if h % 4 == 3:
                        last.then_inc(proj_made, 1)
            pe.wait_ge(proj_act, 2)
            pe.wait_ge(proj_dve, 2)
            for l in range(TJ):
                last = mm(bank[0][0:D, 0:D], q4[:, l, :, :].rearrange("p h b -> p (h b)"),
                          k4[:, l, :, :].rearrange("p h b -> p (h b)"), start=(l == 0), stop=(l == TJ - 1))
            last.then_inc(score_made, 1)
            pe.wait_ge(proj_act, 3)
            pe.wait_ge(proj_dve, 3)
            for l in range(TJ):
                last = nc.tensor.transpose(bank[1 + l // 4][0:D, (l % 4) * P:(l % 4 + 1) * P],
                                           v4[:, l, :, :].rearrange("p h b -> p (h b)"), ident)
                if l % 4 == 3:
                    last.then_inc(vt_made, 1)
            pe.wait_ge(att_ready, 1)
            nc.tensor.transpose(bank[0][0:D, D:2 * D], att[:, :], ident[0:D, 0:D]).then_inc(att_turned, 1)
            pe.wait_ge(att_t_ready, 1)
            pe.wait_ge(vt_act, 2)
            pe.wait_ge(vt_dve, 2)
            pe.wait_ge(proj_act, 3 + HEADS)
            for l in range(TJ):
                last = mm(bank[(7, 1)[l // 8]][:, (l % 8) * D:(l % 8 + 1) * D], vt[:, l, :], att_t[:, :], start=True, stop=True)
                if l % 8 == 7:
                    last.then_inc(o_made, 1)
            pe.wait_ge(dma["wo"], 16)
            pe.wait_ge(o_gated, 2)
            for q in range(2):
                rows = slice(q * D, (q + 1) * D)
                for h in range(HEADS):
                    last = mm(bank[(0, 2)[q]][:, 0:P], wo_diag[rows, h, :], o4[rows, h, :, :].rearrange("p l b -> p (l b)"),
                              start=(h == 0), stop=(h == HEADS - 1))
                last.then_inc(wo_made, 1)
            pe.wait_ge(wo_act, 1)
            nc.tensor.transpose(bank[3][:, 0:P], wo_out[:, 0, :], ident)
            pe.wait_ge(wo_dve, 1)
            nc.tensor.transpose(bank[3][:, P:2 * P], wo_out[:, 1, :], ident).then_inc(t2_made, 1)

            pe.wait_ge(x_norm, 2)
            for j in range(J):
                last = nc.tensor.transpose(bank[4][:, j * P:(j + 1) * P], xn[:, j, :, :].rearrange("p k d -> p (k d)"), ident)
            last.then_inc(x2_turned, 1)
            pe.wait_ge(dma["late"], 16)
            pe.wait_ge(x2_kept, 2)
            for j in range(J):
                last = mm(bank[7][:, j * E:(j + 1) * E], x2_one[:, j * P:(j + 1) * P], wr, start=True, stop=True)
            last.then_inc(logit_made, 1)
            pe.wait_ge(comb_ready, 2)
            for j in range(J):
                last = nc.tensor.transpose(bank[1][:, j * P:(j + 1) * P], comb[:, j, :, :].rearrange("p k e -> p (k e)"), ident)
            last.then_inc(c_turned, 1)
            pe.wait_ge(c_kept, 1)
            mm(bank[4][0:D, :], b2e, c_t[0:D, :], start=True, stop=False)
            pe.wait_ge(c_split, 1)
            pe.wait_ge(x_split, 3)
            pe.wait_ge(fold_ready, 1)
            pe.wait_ge(dma["w2e"], 16)

            def second_layer(i):
                pe.wait_ge(h_gated, 2 * i + 2)
                for k in range(2):
                    e = 2 * i + k
                    last = mm(bank[4][k * D:(k + 1) * D, :], w2e[:, e, :], hg[:, e % 4, :], start=(e == 1), stop=(e >= E - 2))
                last.then_inc(h_used, 1)

            for i in range(E // 2):
                for e in (2 * i, 2 * i + 1):
                    if e % 8 == 0:
                        pe.wait_ge(w1_split, e // 8 + 1)
                    if e >= 4:
                        pe.wait_ge(h_gated, e - 3)
                    mm(bank[(3, 5, 6, 7)[e % 4]][:, :], fold_r[:, e:e + 1].to_broadcast([P, P]), c_hl[:, :],
                       start=True, stop=True).then_inc(c_spread, 1)
                    if e >= 2:
                        pe.wait_ge(h_relu, e - 1)
                    mm(bank[(0, 2)[e % 2]][:, :], w1_hl[:, e, :], x_ab[:, 0, :], start=True, stop=False)
                    mm(bank[(0, 2)[e % 2]][:, :], w1_hl[:, e, :], x_ab[:, 1, :], start=False, stop=True).then_inc(h_made, 1)
                if i >= 1:
                    second_layer(i - 1)
            second_layer(E // 2 - 1)

            def fold_rows(dst, made):
                for j in range(J):
                    last = mm(bank[dst][:, j * D:(j + 1) * D], half[:, j * P:(j + 1) * P], fold, start=True, stop=True)
                last.then_inc(made, 1)

            pe.wait_ge(moe_kept, 1)
            fold_rows(0, t3_made)
            pe.wait_ge(x_norm, 3)
            for j in range(J):
                last = nc.tensor.transpose(bank[1][:, j * P:(j + 1) * P], xn[:, j, :, :].rearrange("p k d -> p (k d)"), ident)
            last.then_inc(x3_turned, 1)
            pe.wait_ge(wc_ready, 1)
            pe.wait_ge(xp_top, 1)
            pe.wait_ge(xp_low, 1)
            for i in range(PAIRS):
                r, lag = i % 2, 2 * i * B
                k = P if i < PAIRS - 1 else D
                if i == 1:
                    pe.wait_ge(total_ready, 1)
                    mm(bank[2][D:P, :].rearrange("p (t b) -> p t b", b=B), w_total[:, :],
                       total[:, :].unsqueeze(1).to_broadcast([D, T, B]), start=True, stop=False)
                last = mm(bank[2][r * D:(r + 1) * D, lag:N], wc[0:k, i, :], xp[0:k, 0:N - lag], start=(i == 0), stop=(i >= PAIRS - 2))
            last.then_inc(conv_made, 1)
            pe.wait_ge(conv_kept, 1)
            fold_rows(3, t4_made)
            pe.wait_ge(x_norm, 4)
            for j in range(J):
                last = nc.tensor.transpose(bank[5][0:D, j * P:(j + 1) * P], xn[:, j, 0, :], ident)
            last.then_inc(x4_turned, 1)
            pe.wait_ge(x4_kept, 1)
            mm(bank[6][:, :], wi_t, x4_t[:, :], start=True, stop=True).then_inc(ffn_made, 1)
            pe.wait_ge(dma["wr_t"], 16)
            pe.wait_ge(ws_kept, 1)
            pe.wait_ge(mask_ready, 1)
            for l in range(NL):
                acc = bank[(7, 0)[l]][:, :]
                mm(acc, br[:, l, :], mask_t[:, :], start=True, stop=False)
                pe.wait_ge(ffn_relu, l + 1)
                mm(acc, ws_t[:, l, :], hf[:, l, :], start=False, stop=False)
                for e in range(NE):
                    n = l * NE + e
                    pe.wait_ge(hm_ready, n + 1)
                    last = mm(acc, wr_t[:, n, :], hm[:, n % 4, :], start=False, stop=(e == NE - 1))
                    last.then_inc(hm_used, 1)
            pe.wait_ge(ffn_relu, NL + 1)
            for j in range(J):
                last = mm(bank[1][:, j * D:(j + 1) * D], hf[:, NL, j * P:(j + 1) * P], wo2_t, start=True, stop=True)
            last.then_inc(t5_made, 1)


def table(names, rows):
    import numpy as np

    wide = np.zeros((P, sum(c for _, c in names.values())), np.float32)
    at = 0
    for name, (r, c) in names.items():
        wide[0:r, at:at + c] = rows[name]
        at += c
    return wide


def laid_out(x, w):
    import numpy as np

    def twice(a):
        return np.concatenate([a, a])

    def every_row(a, r=P):
        return np.broadcast_to(a.reshape(1, -1), (r, a.size))

    head = np.arange(D) // B
    t = np.arange(N) // B
    last = np.float32(NP - 1)
    c = dict(ident=np.eye(P, dtype=np.float32), fold=twice(np.eye(D, dtype=np.float32)),
             expert_no=every_row(np.arange(E, dtype=np.float32)), part_no=np.arange(P, dtype=np.float32)[:, None],
             off_head=np.where(head[:, None] == head[None, :], 0.0, -1e30).astype(np.float32),
             grid=np.stack([(t // NP).astype(np.float32) / last, (t % NP).astype(np.float32) / last, np.ones(N, np.float32)]))
    c["pos_w1"] = np.concatenate([w["L0_tok_W1"], w["L0_tok_b1"][None]])
    c["pos_w2"] = np.concatenate([w["L0_tok_W2"], w["L0_tok_b2"][None], w["L0_tok_bp"][None]])
    c["gamma"] = twice(w["L0_attn_gamma"])[:, None]
    c["beta"] = twice(w["L0_attn_beta"])[:, None]
    c["bg"] = np.concatenate([w["L0_attn_bg"].reshape(HEADS, HC).T] * J)
    c["bo_row"] = every_row(w["L0_attn_bo"])
    c["route"] = every_row(w["L1_ffn_route_id"]).view(np.float32)
    c["wr"] = np.concatenate([w["L0_ffn_Wr"], w["L0_ffn_br"][None]])
    c["b1_t"] = w["L0_ffn_b1"].T
    c["b2e"] = w["L0_ffn_b2"]
    c["w2c"] = twice(w["L1_attn_W2"])
    mw = w["L1_attn_memory_weights"]
    taps = np.zeros((PAIRS + 1, 2, D), np.float32)
    taps[0:PAIRS - 1] = mw[0:TAPS].reshape(PAIRS - 1, 2, D)
    taps[PAIRS - 1, 0] = mw[TAPS]
    taps[PAIRS, :] = mw[0]
    c["mw_t"] = taps.reshape(PAIRS + 1, P).T
    c["w1c"] = w["L1_attn_W1"]
    c["bias_row"] = every_row(w["L1_attn_bias"])
    c["wi_t"] = w["L1_ffn_Wi"].T
    c["bi"] = w["L1_ffn_bi"][:, None]
    c["bs"] = w["L1_ffn_bs"][:, 0].T
    c["ws"] = w["L1_ffn_Ws"][:, 0].transpose(2, 0, 1).reshape(HID, NL * HID)
    c["br"] = w["L1_ffn_br"].transpose(1, 0, 2).reshape(NE, NL * HID)
    c["wo2_t"] = w["L1_ffn_Wo"].T
    c["bo2_row"] = every_row(w["L1_ffn_bo"])

    qkvg = np.zeros((2, D, 4, HEADS, 2, HC), np.float32)
    for m, n in enumerate("qkvg"):
        for r in range(2):
            qkvg[r, :, m, :, r, :] = w["L0_attn_W" + n].reshape(D, HEADS, HC)
    wo = np.zeros((2, 2, HC, HEADS, 2, D), np.float32)
    for r in range(2):
        wo[:, r, :, :, r, :] = w["L0_attn_Wo"].reshape(HEADS, HC, D).transpose(1, 0, 2)
    patches = x.reshape(B, CH, NP, PATCH, NP, PATCH).transpose(1, 3, 5, 2, 4, 0).reshape(KB, P, N)
    return dict(
        early=table(EARLY, c), late=table(LATE, c),
        patches=patches.transpose(1, 0, 2), wp=w["L0_tok_Wp"].reshape(KB, P, D).transpose(1, 0, 2),
        qkvg=qkvg.reshape(P, 4, HEADS, D), wo_diag=wo.reshape(P, HEADS, P),
        w1=w["L0_ffn_W1"].transpose(1, 0, 2), w2e=w["L0_ffn_W2"].transpose(1, 0, 2),
        wr_t=w["L1_ffn_Wr"].transpose(3, 0, 1, 2).reshape(HID, NL * NE, HID))


def kernel(**inputs):
    import numpy as _np
    import concourse.bacc as _bacc
    from concourse import mybir as _mybir
    from concourse.bass_utils import run_bass_kernel_spmd as _run

    nc = _bacc.Bacc("TRN2", target_bir_lowering=False, num_devices=1)
    arrays, aps = {}, {}
    inputs = {name: _np.asarray(a) for name, a in inputs.items()}
    for name, a in laid_out(inputs.pop("x"), inputs).items():
        a = _np.ascontiguousarray(a)
        arrays[f"in_{name}"] = a
        aps[name] = nc.dram_tensor(f"in_{name}", a.shape, _mybir.dt.from_np(a.dtype), kind="ExternalInput").ap()
    out = nc.dram_tensor("out", (P, J, D), F32, kind="ExternalOutput").ap()
    build_tower(nc, aps, out)
    r = _run(nc, [arrays], core_ids=[0])
    return r.results[0]["out"].reshape(TJ, B, J, D).transpose(1, 2, 0, 3).reshape(B, T, D)
```

```python
from contextlib import ExitStack

import concourse.bass as bass
from concourse import mybir

F32 = mybir.dt.float32
F32R = mybir.dt.float32r
BF16 = mybir.dt.bfloat16
I32 = mybir.dt.int32
U32 = mybir.dt.uint32
ALU = mybir.AluOpType
ACT = mybir.ActivationFunctionType
AX = mybir.AxisListType

P = 128
B, CH, IMG, PATCH = 8, 3, 128, 16
NP = IMG // PATCH
T = NP * NP
N = B * T
J = N // P
TJ = T // J
D = 64
HEADS, HC = 8, 32
E, HID = 64, 128
TAPS = 40
PAIRS = TAPS // 2 + 1
NL, NE = 2, 16
EPS = 1e-5
SCALE = 1.0 / (HC ** 0.5) / (T ** 0.5)

POS = dict(grid=(3, N), pos_w1=(3, D))
EARLY = dict(ident=(P, P), fold=(P, D), pos_w2=(D + 2, D), gamma=(P, 1), beta=(P, 1),
             bg=(P, HEADS), expert_no=(P, E), off_head=(D, D), part_no=(P, 1), bo_row=(P, D))
LATE = dict(route=(P, T), wr=(D + 1, E), b1_t=(HID, E), b2e=(E, D), w2c=(P, D), mw_t=(P, PAIRS + 1), w1c=(D, D),
            bias_row=(P, D), wi_t=(D, HID), bi=(HID, 1), bs=(HID, NL), ws=(HID, NL * HID), br=(NE, NL * HID),
            wo2_t=(HID, D), bo2_row=(P, D))
KB = CH * PATCH * PATCH // P

PAIR_BANKS = (3, 5, 6, 4, 1, 7)
RING = len(PAIR_BANKS)
SUM_PAIR = E // 2 - RING
SUM_BANK = PAIR_BANKS[SUM_PAIR % RING]
PE_PAIRS = 11
HALVES = (slice(0, N // 2), slice(N // 2, N))
X2_BANKS, X3_BANKS, X4_BANKS = (4, 6), (1, 4), (5, 6)
O_BANKS = (7, 6, 1, 4)
WI_BANKS = (1, 4)
FFN_BANKS = (7, 0)
GATE_STEP = 4
TURN_STEP = 3
PEELED = 2
WARM = dict(start=9, embedding=3, norm_0=9, turned_0=4, softmax=1, att_turned=3, gating=1, norm_1=6,
            turned_1=4, norm_2=10, turned_2=2, filter=1, norm_3=2, turned_3=1, layer=4)


def build_tower(nc, I, out):
    with ExitStack() as ctx:
        def sb(name, shape, dt=F32):
            return ctx.enter_context(nc.sbuf_tensor(name, shape, dt))

        def sem(name):
            return ctx.enter_context(nc.semaphore(name))

        bank = [ctx.enter_context(nc.psum_tensor(f"bank{i}", [P, 512], F32)) for i in range(8)]

        gates_dram = nc.dram_tensor("gates_dram", (E, N), F32, kind="Internal")

        pos_table = sb("pos_table", [3, N + D])
        early = sb("early", [P, sum(c for _, c in EARLY.values())])
        late = sb("late", [P, sum(c for _, c in LATE.values())])

        def part(tile, table, name):
            at = 0
            for n, (rows, cols) in table.items():
                if n == name:
                    return tile[0:rows, at:at + cols]
                at += cols

        ident = part(early, EARLY, "ident")
        fold = part(early, EARLY, "fold")
        grid = part(pos_table, POS, "grid")
        pos_w1 = part(pos_table, POS, "pos_w1")
        pos_w2 = part(early, EARLY, "pos_w2")
        gamma = part(early, EARLY, "gamma")
        beta = part(early, EARLY, "beta")
        bg = part(early, EARLY, "bg")
        expert_no = part(early, EARLY, "expert_no")
        off_head = part(early, EARLY, "off_head")
        part_no = part(early, EARLY, "part_no")[0:NE]
        bo_row = part(early, EARLY, "bo_row")
        route = part(late, LATE, "route").bitcast(I32)
        wr = part(late, LATE, "wr")
        b1_t = part(late, LATE, "b1_t")
        b2e = part(late, LATE, "b2e")
        w2c = part(late, LATE, "w2c")
        mw_t = part(late, LATE, "mw_t")
        w1c = part(late, LATE, "w1c")
        bias_row = part(late, LATE, "bias_row")
        wi_t = part(late, LATE, "wi_t")
        bi = part(late, LATE, "bi")
        bs = part(late, LATE, "bs")
        ws = part(late, LATE, "ws")
        br = part(late, LATE, "br").rearrange("e (l o) -> e l o", l=NL)
        wo2_t = part(late, LATE, "wo2_t")
        bo2_row = part(late, LATE, "bo2_row")
        wide = sb("wide", [P, 8 * N])
        patches = wide[:, 0:KB * N].rearrange("p (k n) -> p k n", k=KB)
        wp = sb("wp", [P, KB, D])
        zeros = sb("zeros", [P, N], BF16)
        pos_hid = sb("pos_hid", [D + 2, N])
        room = sb("room", [P, 5 * TJ * D])
        emb_half = room[:, 9 * N:10 * N]
        h0b = sb("h0b", [P, J, D])
        h1 = sb("h1", [P, J, D])
        h2b = sb("h2b", [P, J, D])
        h3b = sb("h3b", [P, J, D])
        h4 = sb("h4", [P, J, D])
        stats = sb("stats", [P, J, 6])
        mean_var = sb("mean_var", [P, J, 2])
        std = sb("std", [P, J])
        rstd = sb("rstd", [P, J])
        eps = sb("eps", [P, 2])
        table_turn = sb("table_turn", [P, 2])
        centred = sb("centred", [P, J, D])
        xn = sb("xn", [P, J, D])
        mn_t = sb("mn_t", [P, 2, P])
        neg_bg = sb("neg_bg", [P, HEADS])
        w_qkvg = sb("w_qkvg", [P, 4, HEADS, D])
        q4 = room[:, 0 * N:2 * N].rearrange("p (l h b) -> p l h b", l=TJ, h=HEADS)
        k4 = room[:, 2 * N:4 * N].rearrange("p (l h b) -> p l h b", l=TJ, h=HEADS)
        v4 = room[:, 4 * N:6 * N].rearrange("p (l h b) -> p l h b", l=TJ, h=HEADS)
        gexp = sb("gexp", [P, HEADS, TJ, B])
        g4 = sb("g4", [P, HEADS, TJ, B])
        vt = room[0:D, 6 * N:10 * N].rearrange("p (l c) -> p l c", l=TJ)
        sm = sb("sm", [D, D])
        sm_max = sb("sm_max", [D, 1])
        sm_bias = sb("sm_bias", [D, 1])
        sm_exp = sb("sm_exp", [D, D])
        sm_sum = sb("sm_sum", [D, 1])
        sm_rec = sb("sm_rec", [D, 1])
        att = sb("att", [D, D])
        att_t = sb("att_t", [D, D])
        o4 = gexp
        wo_diag = sb("wo_diag", [P, HEADS, J * D])
        x2_one = sb("x2_one", [D + 1, N])
        x_ab = sb("x_ab", [P, 2, N], F32R)
        w1_raw = sb("w1_raw", [P, E // 2, HID])
        w1_hl = sb("w1_hl", [P, E, HID], F32R)
        w2e = sb("w2e", [HID, E, D])
        top8 = sb("top8", [P, J, 8])
        top_i = sb("top_i", [P, J, 8], U32)
        top_f = sb("top_f", [P, 2, J])
        gap = sb("gap", [P, J])
        gap_exp = sb("gap_exp", [P, J])
        gate_sum = sb("gate_sum", [P, J])
        gate = sb("gate", [P, 2, J])
        chosen = sb("chosen", [P, 2, J, E])
        comb = sb("comb", [P, J, E])
        gates_sb = room[:, 0:RING * N].rearrange("p (i n) -> p i n", i=RING)
        c_t = room[0:D, 9 * N:10 * N]
        hb = wide[:, 0:4 * N].rearrange("p (u n) -> p u n", u=4)
        prod = wide[:, 4 * N:6 * N].rearrange("p (i n) -> p i n", i=2)
        half = sb("half", [P, N])
        mw_rel = sb("mw_rel", [P, PAIRS])
        wc = sb("wc", [P, PE_PAIRS, D])
        x_taps = prod
        w_total = sb("w_total", [D, D])
        xp = sb("xp", [P, B + N])
        total = sb("total", [D, B])
        route_f = sb("route_f", [P, NP, B])
        route_x = sb("route_x", [P, N])
        mask_t = sb("mask_t", [NE, N])
        wr_t = w1_raw
        ws_t = sb("ws_t", [HID, NL, HID])
        x4_t = room[0:D, 8 * N:9 * N]
        hf = wide[:, 4 * N:7 * N].rearrange("p (l n) -> p l n", l=NL + 1)
        hm = wide[:, 0:4 * N].rearrange("p (u n) -> p u n", u=4)

        dma = {n: sem("dma_" + n) for n in ("pos", "early", "late", "wp", "qkvg", "wo", "w2e", "wr_t", "gates_out", "out")}
        dma_x = [sem(f"dma_x{k}") for k in range(KB // 2)]
        dma_gates = [sem(f"dma_gates{u}") for u in range(RING)]
        dma_w1 = [sem(f"dma_w1_{k}") for k in range(8)]
        zeroed = sem("zeroed")
        pool_step = sem("pool_step")
        dve_step = sem("dve_step")
        pos_made = sem("pos_made")
        pos_relu = sem("pos_relu")
        emb_made = sem("emb_made")
        emb_kept = sem("emb_kept")
        tok_made = sem("tok_made")
        var_ready = sem("var_ready")
        std_ready = sem("std_ready")
        x_norm = sem("x_norm")
        x1_turned = sem("x1_turned")
        mn_a = sem("mn_a")
        proj_made = sem("proj_made")
        proj_act = sem("proj_act")
        score_made = sem("score_made")
        vt_made = sem("vt_made")
        vt_act = sem("vt_act")
        vt_dve = sem("vt_dve")
        sm_bias_ready = sem("sm_bias_ready")
        sm_exp_ready = sem("sm_exp_ready")
        att_ready = sem("att_ready")
        att_turned = sem("att_turned")
        att_t_ready = sem("att_t_ready")
        o_made = sem("o_made")
        o_gated = sem("o_gated")
        h1_made = sem("h1_made")
        x2_turned = sem("x2_turned")
        x2_kept = sem("x2_kept")
        x_split = sem("x_split")
        x_high = sem("x_high")
        ws_kept = sem("ws_kept")
        wr_summed = sem("wr_summed")
        logit_made = sem("logit_made")
        table_step = sem("table_step")
        gap_ready = sem("gap_ready")
        gap_exp_ready = sem("gap_exp_ready")
        comb_ready = sem("comb_ready")
        c_turned = sem("c_turned")
        c_kept = sem("c_kept")
        w1_split = sem("w1_split")
        h_made = sem("h_made")
        h_relu = sem("h_relu")
        out_made = sem("out_made")
        prod_ready = sem("prod_ready")
        acc_ready = sem("acc_ready")
        logits_read = sem("logits_read")
        t3_made = sem("t3_made")
        x3_turned = sem("x3_turned")
        xp_top = sem("xp_top")
        xp_low = sem("xp_low")
        total_ready = sem("total_ready")
        wc_ready = sem("wc_ready")
        taps_ready = sem("taps_ready")
        conv_made = sem("conv_made")
        conv_kept = sem("conv_kept")
        t4_made = sem("t4_made")
        x4_turned = sem("x4_turned")
        x4_kept = sem("x4_kept")
        mask_ready = sem("mask_ready")
        ffn_made = sem("ffn_made")
        ffn_relu = sem("ffn_relu")
        hm_ready = sem("hm_ready")
        hm_used = sem("hm_used")
        t5_made = sem("t5_made")
        h4_ready = sem("h4_ready")
        h_kept = sem("h_kept")
        h1_kept = sem("h1_kept")

        block = ctx.enter_context(nc.Block())

        @block.sync
        def _(sp):
            sp.dma_start(wp[:, :, :], I["wp"]).then_inc(dma["wp"], 16)
            for k in range(KB // 2):
                sp.dma_start(patches[:, 2 * k:2 * k + 2, :], I["patches"][:, 2 * k:2 * k + 2, :]).then_inc(dma_x[k], 16)
            sp.dma_start(early[:, :], I["early"]).then_inc(dma["early"], 16)
            sp.dma_start(w_qkvg[:, :, :, :], I["qkvg"]).then_inc(dma["qkvg"], 16)

            def load_w1(k):
                if k >= 4:
                    sp.wait_ge(w1_split, k - 3)
                for r in range(2):
                    sp.dma_start(w1_raw[r * D:(r + 1) * D, (k % 4) * 8:(k % 4 + 1) * 8, :],
                                 I["w1"][:, 8 * k:8 * k + 8, :]).then_inc(dma_w1[k], 16)

            for k in range(4):
                load_w1(k)
            sp.dma_start(wo_diag[:, :, :], I["wo_diag"]).then_inc(dma["wo"], 16)
            sp.dma_start(late[:, :], I["late"]).then_inc(dma["late"], 16)
            sp.dma_start(w2e[:, :, :], I["w2e"]).then_inc(dma["w2e"], 16)
            for k in range(4, 8):
                load_w1(k)

            def spread(i, u, used):
                if used is not None:
                    sp.wait_ge(prod_ready, used)
                sp.dma_start(gates_sb[:, u, :], gates_dram.ap()[bass.ds(i * 2, 2), :].unsqueeze(1).to_broadcast([2, D, N])).then_inc(dma_gates[u], 16)

            sp.wait_ge(c_kept, 1)
            sp.dma_start(gates_dram.ap(), c_t[:, :]).then_inc(dma["gates_out"], 16)
            sp.wait_ge(dma["gates_out"], 16)
            for i in range(RING):
                spread(i, i, None)
            sp.wait_ge(w1_split, 8)
            sp.dma_start(wr_t[:, :, :], I["wr_t"]).then_inc(dma["wr_t"], 16)
            with sp.Fori(1, E // 2 // RING) as g:
                for u in range(RING):
                    spread(g * RING + u, u, g * RING + (u - RING + 1))
            for i in range(E // 2 // RING * RING, E // 2):
                spread(i, i % RING, i - RING + 1)
            sp.wait_ge(h4_ready, 1)
            sp.dma_start(out, h4[:, :, :]).then_inc(dma["out"], 16)
            sp.wait_ge(dma["out"], 16)

        @block.gpsimd
        def _(pool):
            steps = [0]

            def kept(ins):
                steps[0] += 1
                ins.then_inc(pool_step, 1)
                pool.wait_ge(pool_step, steps[0])

            filled = [0]

            def fill(tile, value):
                filled[0] += 1
                nc.gpsimd.memset(tile, value).then_inc(zeroed, 1)
                pool.wait_ge(zeroed, filled[0])

            fill(zeros[:, :], 0.0)
            fill(pos_hid[D:D + 2, :], 1.0)
            fill(eps[:, 0:1], EPS)
            fill(eps[:, 1:2], EPS * EPS)
            fill(x2_one[D:D + 1, :], 1.0)
            fill(xp[D:P, 0:B], 0.0)

            def split_w1(k):
                es = slice(k * E // 8, (k + 1) * E // 8)
                raw = slice((k % 4) * 8, (k % 4 + 1) * 8)
                pool.wait_ge(dma_w1[k], 32)
                kept(nc.gpsimd.tensor_scalar(w1_hl[:, es, :], w1_raw[:, raw, :], 1.0, 0.0, ALU.mult, ALU.add))
                nc.gpsimd.tensor_tensor(w1_hl[D:P, es, :], w1_raw[D:P, raw, :], w1_hl[D:P, es, :].bitcast(F32),
                                        ALU.subtract).then_inc(w1_split, 1)
                pool.wait_ge(w1_split, k + 1)

            pool.wait_ge(dma["late"], 16)
            kept(nc.gpsimd.tensor_tensor(mw_rel[:, :], mw_t[:, 0:PAIRS], mw_t[:, PAIRS:PAIRS + 1].to_broadcast([P, PAIRS]), ALU.subtract))
            kept(nc.gpsimd.tensor_tensor(wc[:, :, :], mw_rel[:, 0:PE_PAIRS].unsqueeze(2).to_broadcast([P, PE_PAIRS, D]),
                                         w2c.unsqueeze(1).to_broadcast([P, PE_PAIRS, D]), ALU.mult))
            kept(nc.gpsimd.tensor_copy(wc[0:D, 0, :], w1c))
            nc.gpsimd.tensor_tensor(w_total[:, :], mw_t[0:D, PAIRS:PAIRS + 1].to_broadcast([D, D]), w2c[0:D],
                                    ALU.mult).then_inc(wc_ready, 1)
            pool.wait_ge(wc_ready, 1)
            for k in range(8):
                split_w1(k)

            pool.wait_ge(dma["wr_t"], 16)
            pool.wait_ge(ws_kept, 1)
            for q in range(NL * NE // 4):
                ns = slice(4 * q, 4 * q + 4)
                nc.gpsimd.tensor_tensor(wr_t[:, ns, :], wr_t[:, ns, :], ws_t[:, q // (NE // 4), :].unsqueeze(1).to_broadcast([HID, 4, HID]),
                                        ALU.add).then_inc(wr_summed, 1)
                pool.wait_ge(wr_summed, q + 1)

        @block.scalar
        def _(act):
            A = nc.scalar.activation

            def root(n, scale, which):
                act.wait_ge(var_ready, J * (n + 1))
                A(std[:, :], mean_var[:, :, 1], ACT.Sqrt, bias=eps[:, which:which + 1], scale=scale).then_inc(std_ready, 1)

            def load_table(func, k):
                A(table_turn[:, k:k + 1], eps[:, 0:1], func).then_inc(table_step, 1)

            act.dma_start(pos_table[:, :], I["pos"]).then_inc(dma["pos"], 16)
            act.wait_ge(zeroed, 6)
            load_table(ACT.Sqrt, 0)

            act.wait_ge(pos_made, 1)
            A(pos_hid[0:D, :], bank[3][0:D, :], ACT.Relu).then_inc(pos_relu, 1)
            act.wait_ge(emb_made, 1)
            for cols in HALVES:
                A(emb_half[:, cols], bank[0][:, cols], ACT.Copy).then_inc(emb_kept, 1)
            root(0, 1.0 + EPS, 1)
            load_table(ACT.Exp, 1)
            act.wait_ge(x1_turned, 1)
            A(mn_t[:, :, :].rearrange("p q n -> p (q n)"), bank[4][:, 0:2 * P], ACT.Identity, bias=beta, scale=gamma).then_inc(mn_a, 1)
            act.wait_ge(x_norm, 1)
            for h in range(HEADS):
                act.wait_ge(proj_made, 1 + h // 4)
                A(gexp[:, h, :, :].rearrange("p l b -> p (l b)"), bank[6 + h // 4][:, (h % 4) * P:(h % 4 + 1) * P], ACT.Exp,
                  bias=neg_bg[:, h:h + 1], scale=-1.0).then_inc(proj_act, 1)
            for m, dst in enumerate((q4, k4, v4)):
                for r in range(2):
                    act.wait_ge(proj_made, 3 + 2 * m + r)
                    A(dst[:, :, 4 * r:4 * r + 4, :].rearrange("p l h b -> p h l b"),
                      bank[2 * m + r][:, :].rearrange("p (h l b) -> p h l b", h=4, b=B), ACT.Copy).then_inc(proj_act, 1)
            act.wait_ge(sm_bias_ready, 1)
            A(sm_exp[:, :], sm[:, :], ACT.Exp, bias=sm_bias[:, 0:1], scale=SCALE, accum_out=sm_sum[:, 0:1]).then_inc(sm_exp_ready, 1)
            for k in (0, 2):
                act.wait_ge(vt_made, k + 1)
                A(vt[:, 4 * k:4 * k + 4, :].rearrange("p l c -> p (l c)"), bank[1 + k][0:D, :], ACT.Copy).then_inc(vt_act, 1)
            act.wait_ge(table_step, 1)
            load_table(ACT.Sqrt, 0)
            root(1, 1.0, 0)
            act.wait_ge(table_step, 2)
            load_table(ACT.Exp, 1)
            act.wait_ge(x_norm, 2)
            A(h1[:, :, :].rearrange("p j d -> p (j d)"), bank[3][:, 0:J * D], ACT.Copy).then_inc(h1_kept, 1)

            for k, cols in enumerate(HALVES):
                act.wait_ge(x2_turned, k + 1)
                A(x_ab[:, 0, cols], bank[X2_BANKS[k]][:, HALVES[0]], ACT.Copy).then_inc(x_high, 1)
            for k, cols in enumerate(HALVES):
                act.wait_ge(x_split, k + 1)
                A(x2_one[0:D, cols], bank[X2_BANKS[k]][0:D, HALVES[0]], ACT.Copy).then_inc(x2_kept, 1)

            act.wait_ge(dma["late"], 16)

            def relu(e, u, pairs_out):
                act.wait_ge(h_made, e + 1)
                if pairs_out is not None:
                    act.wait_ge(out_made, pairs_out)
                A(hb[:, u, :], bank[(0, 2)[u % 2]][:, :], ACT.Relu, bias=b1_t[:, bass.ds(e, 1)]).then_inc(h_relu, 1)

            for e in range(4 * PEELED):
                if e == GATE_STEP:
                    act.wait_ge(gap_ready, 1)
                    A(gap_exp[:, :], gap[:, :], ACT.Exp).then_inc(gap_exp_ready, 1)
                if e == 2 * TURN_STEP + 1:
                    act.wait_ge(c_turned, 1)
                    A(c_t[:, :], bank[1][0:D, :], ACT.Copy).then_inc(c_kept, 1)
                relu(e, e % 4, e // 2 - 1 if e >= 4 else None)
            with act.Fori(PEELED, E // 4) as g:
                for u in range(4):
                    relu(g * 4 + u, u, g * 2 + (u // 2 - 1))

            act.wait_ge(table_step, 3)
            load_table(ACT.Sqrt, 0)
            root(2, 1.0, 0)
            for k, cols in enumerate(HALVES):
                act.wait_ge(x3_turned, k + 1)
                A(xp[0:D, cols], bank[X3_BANKS[k]][0:D, HALVES[0]], ACT.Copy).then_inc(xp_top, 1)
            act.wait_ge(conv_made, 1)
            for cols in HALVES:
                A(half[:, cols], bank[2][:, cols], ACT.Copy).then_inc(conv_kept, 1)
            root(3, 1.0, 0)
            for k, cols in enumerate(HALVES):
                act.wait_ge(x4_turned, k + 1)
                A(x4_t[:, cols], bank[X4_BANKS[k]][0:D, HALVES[0]], ACT.Copy).then_inc(x4_kept, 1)
            for k, cols in enumerate(HALVES):
                act.wait_ge(ffn_made, k + 1)
                A(hf[:, 0, cols], bank[WI_BANKS[k]][:, cols], ACT.Relu, bias=bi[:, 0:1]).then_inc(ffn_relu, 1)
            for l in range(NL):
                act.wait_ge(hm_used, (l + 1) * NE)
                for cols in HALVES:
                    A(hf[:, l + 1, cols], bank[FFN_BANKS[l]][:, cols], ACT.Relu, bias=bs[:, l:l + 1]).then_inc(ffn_relu, 1)

        @block.vector
        def _(dve):
            V = nc.vector
            steps = [0]

            def count(ins):
                steps[0] += 1
                ins.then_inc(dve_step, 1)

            def settle():
                dve.wait_ge(dve_step, steps[0])

            def kept(ins):
                count(ins)
                settle()

            def res(b):
                return bank[b][:, 0:J * D].rearrange("p (j d) -> p j d", j=J)

            def keep(n, b, bias, dst):
                V.tensor_tensor(dst[:, :, :], res(b), bias.unsqueeze(1).to_broadcast([P, J, D]), ALU.add).then_inc(h_kept, 1)

            def layer_norm(n, src, dst):
                for j in range(J):
                    count(V.bn_stats(stats[:, j, :], src[:, j, :]))
                settle()
                for j in range(J):
                    V.bn_aggr(mean_var[:, j, :], stats[:, j, :]).then_inc(var_ready, 1)
                dve.wait_ge(var_ready, J * (n + 1))
                kept(V.tensor_tensor(centred[:, :, :], src, mean_var[:, :, 0:1].to_broadcast([P, J, D]), ALU.subtract))
                dve.wait_ge(std_ready, n + 1)
                kept(V.reciprocal(rstd[:, :], std[:, :]))
                V.tensor_tensor(dst, centred[:, :, :], rstd[:, :].unsqueeze(2).to_broadcast([P, J, D]), ALU.mult).then_inc(x_norm, 1)

            dve.wait_ge(dma["early"], 16)
            kept(V.tensor_scalar(neg_bg[:, :], bg, -1.0, None, ALU.mult))

            dve.wait_ge(tok_made, 1)
            layer_norm(0, res(2), xn[:, :, :])
            keep(0, 2, bo_row, h0b)
            dve.wait_ge(proj_act, HEADS)
            kept(V.tensor_scalar(gexp[:, :, :, :], gexp[:, :, :, :], 1.0, None, ALU.add))
            count(V.reciprocal(g4[:, :, :, :], gexp[:, :, :, :]))
            dve.wait_ge(score_made, 1)
            kept(V.tensor_tensor(sm[:, :], bank[0][0:D, 0:D], off_head, ALU.add))
            kept(V.tensor_reduce(sm_max[:, :], sm[:, :], AX.X, ALU.max))
            V.tensor_scalar(sm_bias[:, :], sm_max[:, :], -SCALE, None, ALU.mult).then_inc(sm_bias_ready, 1)
            dve.wait_ge(sm_exp_ready, 1)
            kept(V.reciprocal(sm_rec[:, :], sm_sum[:, :]))
            V.tensor_scalar(att[:, :], sm_exp[:, :], sm_rec[:, 0:1], None, ALU.mult).then_inc(att_ready, 1)
            dve.wait_ge(vt_made, 2)
            V.tensor_copy(vt[:, 4:8, :].rearrange("p l c -> p (l c)"), bank[2][0:D, :]).then_inc(vt_dve, 1)
            dve.wait_ge(att_turned, 1)
            V.tensor_copy(att_t[:, :], bank[0][0:D, D:2 * D]).then_inc(att_t_ready, 1)
            dve.wait_ge(vt_made, 4)
            V.tensor_copy(vt[:, 12:16, :].rearrange("p l c -> p (l c)"), bank[4][0:D, :]).then_inc(vt_dve, 1)
            for k in range(4):
                dve.wait_ge(o_made, k + 1)
                ls = slice(4 * k, 4 * k + 4)
                V.tensor_tensor(o4[:, :, ls, :], bank[O_BANKS[k]][:, 0:4 * D].rearrange("p (l h b) -> p h l b", h=HEADS, b=B),
                                g4[:, :, ls, :], ALU.mult).then_inc(o_gated, 1)
            dve.wait_ge(h1_made, 1)
            dve.wait_ge(x1_turned, 1)
            layer_norm(1, res(3), xn[:, :, :])

            for k, cols in enumerate(HALVES):
                dve.wait_ge(x_high, k + 1)
                V.tensor_tensor(x_ab[:, 1, cols], bank[X2_BANKS[k]][:, HALVES[0]], x_ab[:, 0, cols].bitcast(F32), ALU.subtract).then_inc(x_split, 1)
            dve.wait_ge(logit_made, 1)
            for j in range(J):
                count(V.max(top8[:, j, :], bank[7][:, j * E:(j + 1) * E]))
            settle()
            V.tensor_tensor(gap[:, :], top8[:, :, 1], top8[:, :, 0], ALU.subtract).then_inc(gap_ready, 1)
            for j in range(J):
                V.max_index(top_i[:, j, :], top8[:, j, :], bank[7][:, j * E:(j + 1) * E]).then_inc(logits_read, 1)
            dve.wait_ge(logits_read, J)
            kept(V.tensor_copy(top_f[:, :, :].rearrange("p k j -> p j k"), top_i[:, :, 0:2]))
            kept(V.tensor_tensor(chosen[:, :, :, :], top_f[:, :, :].unsqueeze(3).to_broadcast([P, 2, J, E]),
                                 expert_no.unsqueeze(1).unsqueeze(1).to_broadcast([P, 2, J, E]), ALU.is_equal))
            dve.wait_ge(gap_exp_ready, 1)
            kept(V.tensor_scalar(gate_sum[:, :], gap_exp[:, :], 1.0, None, ALU.add))
            kept(V.reciprocal(gate[:, 0, :], gate_sum[:, :]))
            kept(V.tensor_tensor(gate[:, 1, :], gate[:, 0, :], gap_exp[:, :], ALU.mult))
            kept(V.tensor_tensor(chosen[:, :, :, :], chosen[:, :, :, :], gate[:, :, :].unsqueeze(3).to_broadcast([P, 2, J, E]), ALU.mult))
            V.tensor_tensor(comb[:, :, :], chosen[:, 0, :, :], chosen[:, 1, :, :], ALU.add).then_inc(comb_ready, 1)

            dve.wait_ge(dma["late"], 16)
            kept(V.tensor_copy(route_f[:, :, :], route.rearrange("p (b y) -> p y b", b=B)))
            kept(V.tensor_copy(route_x[:, :].rearrange("p (y x b) -> p y x b", y=NP, b=B),
                               route_f[:, :, :].unsqueeze(2).to_broadcast([P, NP, NP, B])))
            V.tensor_scalar(mask_t[:, :], route_x[0:NE, :], part_no, None, ALU.is_equal).then_inc(mask_ready, 1)
            V.tensor_tensor(ws_t[:, :, :], ws.rearrange("p (l o) -> p l o", l=NL), ident.unsqueeze(1).to_broadcast([P, NL, P]),
                            ALU.add).then_inc(ws_kept, 1)
            def gated(i, u, times, k):
                dve.wait_ge(out_made, i + 1)
                dve.wait_ge(dma_gates[u], times * 16)
                V.tensor_tensor(prod[:, k, :], bank[PAIR_BANKS[u]][:, :], gates_sb[:, u, :], ALU.mult).then_inc(prod_ready, 1)

            def summed(i, k):
                dve.wait_ge(prod_ready, i + 1)
                dve.wait_ge(acc_ready, i)
                V.tensor_tensor(half[:, :], half[:, :], prod[:, k, :], ALU.add).then_inc(acc_ready, 1)

            gated(0, 0, 1, 0)
            dve.wait_ge(prod_ready, 1)
            V.tensor_copy(half[:, :], prod[:, 0, :]).then_inc(acc_ready, 1)
            for i in range(1, RING):
                gated(i, i, 1, i % 2)
                summed(i, i % 2)
            with dve.Fori(1, E // 2 // RING) as g:
                for u in range(RING):
                    gated(g * RING + u, u, g + 1, u % 2)
                    summed(g * RING + u, u % 2)
            for i in range(E // 2 // RING * RING, E // 2 - 1):
                gated(i, i % RING, i // RING + 1, i % 2)
                summed(i, i % 2)
            i, u = E // 2 - 1, (E // 2 - 1) % RING
            dve.wait_ge(out_made, i + 1)
            dve.wait_ge(dma_gates[u], (i // RING + 1) * 16)
            for cols in HALVES:
                V.tensor_tensor(prod[:, 1, cols], bank[PAIR_BANKS[u]][:, cols], gates_sb[:, u, cols], ALU.mult).then_inc(prod_ready, 1)

            dve.wait_ge(t3_made, 1)
            layer_norm(2, res(SUM_BANK), xn[:, :, :])
            keep(2, SUM_BANK, bias_row, h2b)
            for k in range(2):
                dve.wait_ge(x3_turned, k + 1)
                V.tensor_copy(xp[D:P, B + k * N // 2:B + (k + 1) * N // 2], bank[X3_BANKS[k]][D:P, HALVES[0]]).then_inc(xp_low, 1)
            dve.wait_ge(xp_top, 2)
            V.tensor_reduce(total[:, :], xp[0:D, 0:N].rearrange("p (t b) -> p b t", b=B), AX.X, ALU.add).then_inc(total_ready, 1)
            dve.wait_ge(wc_ready, 1)
            dve.wait_ge(xp_low, 2)
            for i in range(PE_PAIRS, PAIRS):
                rows, lag, r = P if i < PAIRS - 1 else D, 2 * i * B, i % 2
                sums = x_taps[0:rows, r, lag:N]
                if i < PE_PAIRS + 2:
                    V.tensor_scalar(sums, xp[0:rows, 0:N - lag], mw_rel[0:rows, i:i + 1], None, ALU.mult).then_inc(taps_ready, 1)
                else:
                    dve.wait_ge(taps_ready, i - PE_PAIRS - 1)
                    V.scalar_tensor_tensor(sums, xp[0:rows, 0:N - lag], mw_rel[0:rows, i:i + 1], sums, ALU.mult,
                                           ALU.add).then_inc(taps_ready, 1)
            dve.wait_ge(t4_made, 1)
            layer_norm(3, res(3), xn[:, :, :])
            keep(3, 3, bo2_row, h3b)
            def masked(n, l, e, cols):
                V.scalar_tensor_tensor(hm[:, n % 4, cols], route_x[:, cols], float(e), hf[:, l, cols], ALU.is_equal,
                                       ALU.mult).then_inc(hm_ready, 1)

            for l in range(NL):
                for e in range(NE):
                    n = l * NE + e
                    if n >= 4:
                        dve.wait_ge(hm_used, n - 3)
                    if e == 0:
                        for k, cols in enumerate(HALVES):
                            dve.wait_ge(ffn_relu, 2 * l + k + 1)
                            masked(n, l, e, cols)
                    else:
                        masked(n, l, e, slice(0, N))
            dve.wait_ge(t5_made, 1)
            V.tensor_copy(h4[:, :, :], res(1)).then_inc(h4_ready, 1)

        @block.tensor
        def _(pe):
            mm = nc.tensor.matmul

            def keep_warm(n, b=5):
                for _ in range(n):
                    mm(bank[b][:, :], zeros[:, 0:P], zeros[:, :], start=True, stop=True)

            def turn(banks, made, copies):
                for j in range(J):
                    for r in range(copies):
                        last = mm(bank[banks[j // 2]][r * D:(r + 1) * D, j % 2 * P:(j % 2 + 1) * P], xn[:, j, :], ident, start=True, stop=True)
                    if j % 2 == 1:
                        last.then_inc(made, 1)

            pe.wait_ge(zeroed, 1)
            keep_warm(WARM["start"])
            pe.wait_ge(dma["wp"], 16)
            for k in range(KB):
                if k == 2:
                    pe.wait_ge(dma["pos"], 16)
                    mm(bank[3][0:D, :], pos_w1, grid, start=True, stop=True).then_inc(pos_made, 1)
                if k % 2 == 0:
                    pe.wait_ge(dma_x[k // 2], 16)
                r = k % 2
                last = mm(bank[0][r * D:(r + 1) * D, :], wp[:, k, :], patches[:, k, :], start=(k < 2), stop=(k >= KB - 2))
            last.then_inc(emb_made, 1)
            pe.wait_ge(dma["early"], 16)
            pe.wait_ge(pos_relu, 1)
            pe.wait_ge(zeroed, 2)
            keep_warm(WARM["embedding"])
            for j in range(J):
                if j % 2 == 0:
                    pe.wait_ge(emb_kept, j // 2 + 1)
                dst = bank[2][:, j * D:(j + 1) * D]
                mm(dst, pos_hid[:, j * P:(j + 1) * P], pos_w2, start=True, stop=False)
                last = mm(dst, emb_half[:, j * P:(j + 1) * P], fold, start=False, stop=True)
            last.then_inc(tok_made, 1)

            keep_warm(WARM["norm_0"])
            pe.wait_ge(x_norm, 1)
            for q in range(2):
                last = nc.tensor.transpose(bank[4][:, q * P:(q + 1) * P], xn[:, 2 * q:2 * q + 2, :].rearrange("p r d -> p (r d)"), ident)
            last.then_inc(x1_turned, 1)
            keep_warm(WARM["turned_0"])
            pe.wait_ge(dma["qkvg"], 16)
            pe.wait_ge(mn_a, 1)
            for n, m in enumerate((3, 0, 1, 2)):
                if n == 2:
                    pe.wait_ge(h_kept, 1)
                for h in range(HEADS):
                    for q in range(2):
                        last = mm(bank[2 * m + h // 4][q * D:(q + 1) * D, (h % 4) * P:(h % 4 + 1) * P],
                                  w_qkvg[:, m, h, :], mn_t[:, q, :], start=True, stop=True)
                    if h % 4 == 3:
                        last.then_inc(proj_made, 1)
            pe.wait_ge(proj_act, HEADS + 4)
            for l in range(TJ):
                last = mm(bank[0][0:D, 0:D], q4[:, l, :, :].rearrange("p h b -> p (h b)"),
                          k4[:, l, :, :].rearrange("p h b -> p (h b)"), start=(l == 0), stop=(l == TJ - 1))
            last.then_inc(score_made, 1)
            pe.wait_ge(proj_act, HEADS + 6)
            for l in range(TJ):
                last = nc.tensor.transpose(bank[1 + l // 4][0:D, (l % 4) * P:(l % 4 + 1) * P],
                                           v4[:, l, :, :].rearrange("p h b -> p (h b)"), ident)
                if l % 4 == 3:
                    last.then_inc(vt_made, 1)
            keep_warm(WARM["softmax"])
            pe.wait_ge(att_ready, 1)
            nc.tensor.transpose(bank[0][0:D, D:2 * D], att[:, :], ident[0:D, 0:D]).then_inc(att_turned, 1)
            keep_warm(WARM["att_turned"])
            pe.wait_ge(att_t_ready, 1)
            for l in range(TJ):
                if l % 4 == 0:
                    pe.wait_ge((vt_act, vt_dve)[l // 4 % 2], l // 8 + 1)
                last = mm(bank[O_BANKS[l // 4]][:, (l % 4) * D:(l % 4 + 1) * D], vt[:, l, :], att_t[:, :], start=True, stop=True)
                if l % 4 == 3:
                    last.then_inc(o_made, 1)
            def open_with(dst, kept_h):
                mm(bank[dst][:, 0:J * D], ident, kept_h[:, :, :].rearrange("p j d -> p (j d)"), start=True, stop=False)

            open_with(3, h0b)
            pe.wait_ge(dma["wo"], 16)
            keep_warm(WARM["gating"])
            pe.wait_ge(o_gated, 4)
            for h in range(HEADS):
                last = mm(bank[3][:, 0:J * D], o4[:, h, :, :].rearrange("p l b -> p (l b)"), wo_diag[:, h, :],
                          start=False, stop=(h == HEADS - 1))
            last.then_inc(h1_made, 1)

            keep_warm(WARM["norm_1"])
            pe.wait_ge(x_norm, 2)
            turn(X2_BANKS, x2_turned, 2)
            pe.wait_ge(dma["late"], 16)
            keep_warm(WARM["turned_1"])
            pe.wait_ge(h1_kept, 1)
            pe.wait_ge(x_high, 2)

            def first_layer(e):
                if e % 8 == 0:
                    pe.wait_ge(w1_split, e // 8 + 1)
                if e >= 2:
                    pe.wait_ge(h_relu, e - 1)
                mm(bank[(0, 2)[e % 2]][:, :], w1_hl[:, e, :], x_ab[:, 0, :], start=True, stop=False)
                if e == 0:
                    pe.wait_ge(x_split, 2)
                mm(bank[(0, 2)[e % 2]][:, :], w1_hl[:, e, :], x_ab[:, 1, :], start=False, stop=True).then_inc(h_made, 1)

            def second_layer(i):
                pe.wait_ge(h_relu, 2 * i + 2)
                if i >= RING:
                    pe.wait_ge(prod_ready, i - RING + 1)
                for k in range(2):
                    e = 2 * i + k
                    last = mm(bank[PAIR_BANKS[i % RING]][k * D:(k + 1) * D, :], w2e[:, e, :], hb[:, e % 4, :], start=True, stop=True)
                last.then_inc(out_made, 1)

            pe.wait_ge(dma["w2e"], 16)
            for i in range(E // 2):
                first_layer(2 * i)
                if i == TURN_STEP:
                    pe.wait_ge(comb_ready, 1)
                    for j in range(J):
                        last = nc.tensor.transpose(bank[1][0:D, j * P:(j + 1) * P], comb[:, j, :], ident)
                    last.then_inc(c_turned, 1)
                first_layer(2 * i + 1)
                if i == 0:
                    pe.wait_ge(x2_kept, 2)
                    for j in range(J):
                        last = mm(bank[7][:, j * E:(j + 1) * E], x2_one[:, j * P:(j + 1) * P], wr, start=True, stop=True)
                    last.then_inc(logit_made, 1)
                if i == TURN_STEP + 1:
                    pe.wait_ge(c_kept, 1)
                    pe.wait_ge(logits_read, J)
                if i >= 1:
                    second_layer(i - 1)
                if i == E // 2 - 1:
                    pe.wait_ge(prod_ready, SUM_PAIR + 1)
                    open_with(SUM_BANK, h1)
                    for j in range(J):
                        mm(bank[SUM_BANK][:, j * D:(j + 1) * D], c_t[:, j * P:(j + 1) * P], b2e, start=False, stop=False)
            second_layer(E // 2 - 1)

            def fold_rows(dst, src, last_part, made=None, halves=None, before=0):
                for j in range(J):
                    if halves is not None and j % 2 == 0:
                        pe.wait_ge(halves, before + j // 2 + 1)
                    last = mm(bank[dst][:, j * D:(j + 1) * D], src[:, j * P:(j + 1) * P], fold, start=False, stop=last_part and j == J - 1)
                if last_part:
                    last.then_inc(made, 1)

            pe.wait_ge(acc_ready, E // 2 - 1)
            fold_rows(SUM_BANK, half, False)
            fold_rows(SUM_BANK, prod[:, 1, :], True, t3_made, prod_ready, E // 2 - 1)
            keep_warm(WARM["norm_2"])
            pe.wait_ge(x_norm, 3)
            turn(X3_BANKS, x3_turned, 2)
            keep_warm(WARM["turned_2"])
            pe.wait_ge(wc_ready, 1)
            pe.wait_ge(xp_top, 2)
            pe.wait_ge(xp_low, 2)
            for i in range(PE_PAIRS):
                r, lag = i % 2, 2 * i * B
                if i == 1:
                    pe.wait_ge(total_ready, 1)
                    mm(bank[2][D:P, :].rearrange("p (t b) -> p t b", b=B), w_total[:, :],
                       total[:, :].unsqueeze(1).to_broadcast([D, T, B]), start=True, stop=False)
                mm(bank[2][r * D:(r + 1) * D, lag:N], wc[:, i, :], xp[:, 0:N - lag], start=(i == 0), stop=False)
            pe.wait_ge(taps_ready, PAIRS - PE_PAIRS)
            for i in (PE_PAIRS, PE_PAIRS + 1):
                r, lag = i % 2, 2 * i * B
                last = mm(bank[2][r * D:(r + 1) * D, lag:N], w2c, x_taps[:, r, lag:N], start=False, stop=True)
            last.then_inc(conv_made, 1)
            pe.wait_ge(h_kept, 2)
            open_with(3, h2b)
            keep_warm(WARM["filter"])
            fold_rows(3, half, True, t4_made, conv_kept)
            pe.wait_ge(mask_ready, 1)
            for l in range(NL):
                mm(bank[FFN_BANKS[l]][:, :], br[:, l, :], mask_t[:, :], start=True, stop=False)
            keep_warm(WARM["norm_3"], 2)
            pe.wait_ge(x_norm, 4)
            turn(X4_BANKS, x4_turned, 1)
            keep_warm(WARM["turned_3"], 2)
            for k, cols in enumerate(HALVES):
                pe.wait_ge(x4_kept, k + 1)
                mm(bank[WI_BANKS[k]][:, cols], wi_t, x4_t[:, cols], start=True, stop=True).then_inc(ffn_made, 1)
            pe.wait_ge(wr_summed, NL * NE // 4)
            for l in range(NL):
                acc = bank[FFN_BANKS[l]][:, :]
                keep_warm(WARM["layer"], 2)
                for e in range(NE):
                    n = l * NE + e
                    for k, cols in enumerate(HALVES if e == 0 else (slice(0, N),)):
                        pe.wait_ge(hm_ready, l * (NE + 1) + e + (k if e == 0 else 1) + 1)
                        last = mm(acc[:, cols], wr_t[:, n, :], hm[:, n % 4, cols], start=False, stop=(e == NE - 1))
                    last.then_inc(hm_used, 1)
            pe.wait_ge(h_kept, 3)
            open_with(1, h3b)
            for j in range(J):
                if j % 2 == 0:
                    pe.wait_ge(ffn_relu, 2 * NL + j // 2 + 1)
                last = mm(bank[1][:, j * D:(j + 1) * D], hf[:, NL, j * P:(j + 1) * P], wo2_t, start=False, stop=(j == J - 1))
            last.then_inc(t5_made, 1)


def table(names, rows, height=P):
    import numpy as np

    wide = np.zeros((height, sum(c for _, c in names.values())), np.float32)
    at = 0
    for name, (r, c) in names.items():
        wide[0:r, at:at + c] = rows[name]
        at += c
    return wide


def laid_out(x, w):
    import numpy as np

    def twice(a):
        return np.concatenate([a, a])

    def every_row(a, r=P):
        return np.broadcast_to(a.reshape(1, -1), (r, a.size))

    head = np.arange(D) // B
    t = np.arange(N) // B
    last = np.float32(NP - 1)
    c = dict(ident=np.eye(P, dtype=np.float32), fold=twice(np.eye(D, dtype=np.float32)),
             expert_no=every_row(np.arange(E, dtype=np.float32)), part_no=np.arange(P, dtype=np.float32)[:, None],
             off_head=np.where(head[:, None] == head[None, :], 0.0, -1e30).astype(np.float32),
             grid=np.stack([(t // NP).astype(np.float32) / last, (t % NP).astype(np.float32) / last, np.ones(N, np.float32)]))
    c["pos_w1"] = np.concatenate([w["L0_tok_W1"], w["L0_tok_b1"][None]])
    c["pos_w2"] = np.concatenate([w["L0_tok_W2"], w["L0_tok_b2"][None], w["L0_tok_bp"][None]])
    c["gamma"] = twice(w["L0_attn_gamma"])[:, None]
    c["beta"] = twice(w["L0_attn_beta"])[:, None]
    c["bg"] = np.concatenate([w["L0_attn_bg"].reshape(HEADS, HC).T] * J)
    c["bo_row"] = every_row(w["L0_attn_bo"])
    c["route"] = every_row(w["L1_ffn_route_id"]).view(np.float32)
    c["wr"] = np.concatenate([w["L0_ffn_Wr"], w["L0_ffn_br"][None]])
    c["b1_t"] = w["L0_ffn_b1"].T
    c["b2e"] = w["L0_ffn_b2"]
    c["w2c"] = twice(w["L1_attn_W2"])
    mw = w["L1_attn_memory_weights"]
    taps = np.zeros((PAIRS + 1, 2, D), np.float32)
    taps[0:PAIRS - 1] = mw[0:TAPS].reshape(PAIRS - 1, 2, D)
    taps[PAIRS - 1, 0] = mw[TAPS]
    taps[PAIRS, :] = mw[0]
    c["mw_t"] = taps.reshape(PAIRS + 1, P).T
    c["w1c"] = w["L1_attn_W1"]
    c["bias_row"] = every_row(w["L1_attn_bias"])
    c["wi_t"] = w["L1_ffn_Wi"].T
    c["bi"] = w["L1_ffn_bi"][:, None]
    c["bs"] = w["L1_ffn_bs"][:, 0].T
    c["ws"] = w["L1_ffn_Ws"][:, 0].transpose(2, 0, 1).reshape(HID, NL * HID)
    c["br"] = w["L1_ffn_br"].transpose(1, 0, 2).reshape(NE, NL * HID)
    c["wo2_t"] = w["L1_ffn_Wo"].T
    c["bo2_row"] = every_row(w["L1_ffn_bo"])

    qkvg = np.zeros((2, D, 4, HEADS, 2, HC), np.float32)
    for m, n in enumerate("qkvg"):
        for r in range(2):
            qkvg[r, :, m, :, r, :] = w["L0_attn_W" + n].reshape(D, HEADS, HC)
    wo = np.zeros((J, HC, HEADS, J, D), np.float32)
    for j in range(J):
        wo[j, :, :, j, :] = w["L0_attn_Wo"].reshape(HEADS, HC, D).transpose(1, 0, 2)
    patches = x.reshape(B, CH, NP, PATCH, NP, PATCH).transpose(1, 3, 5, 2, 4, 0).reshape(KB, P, N)
    return dict(
        pos=table(POS, c, 3), early=table(EARLY, c), late=table(LATE, c),
        patches=patches.transpose(1, 0, 2), wp=w["L0_tok_Wp"].reshape(KB, P, D).transpose(1, 0, 2),
        qkvg=qkvg.reshape(P, 4, HEADS, D), wo_diag=wo.reshape(P, HEADS, J * D),
        w1=w["L0_ffn_W1"].transpose(1, 0, 2), w2e=w["L0_ffn_W2"].transpose(1, 0, 2),
        wr_t=w["L1_ffn_Wr"].transpose(3, 0, 1, 2).reshape(HID, NL * NE, HID))


def kernel(**inputs):
    import numpy as _np
    import concourse.bacc as _bacc
    from concourse import mybir as _mybir
    from concourse.bass_utils import run_bass_kernel_spmd as _run

    nc = _bacc.Bacc("TRN2", target_bir_lowering=False, num_devices=1)
    arrays, aps = {}, {}
    inputs = {name: _np.asarray(a) for name, a in inputs.items()}
    for name, a in laid_out(inputs.pop("x"), inputs).items():
        a = _np.ascontiguousarray(a)
        arrays[f"in_{name}"] = a
        aps[name] = nc.dram_tensor(f"in_{name}", a.shape, _mybir.dt.from_np(a.dtype), kind="ExternalInput").ap()
    out = nc.dram_tensor("out", (P, J, D), F32, kind="ExternalOutput").ap()
    build_tower(nc, aps, out)
    r = _run(nc, [arrays], core_ids=[0])
    return r.results[0]["out"].reshape(TJ, B, J, D).transpose(1, 2, 0, 3).reshape(B, T, D)
```
